# Optimizing a Trainium2 kernel written in Bass

```python
import numpy as np
import jax
import jax.numpy as jnp

def _softmax(x, axis=-1):
    return jax.nn.softmax(x, axis=axis)
def _gelu(x):
    return jax.nn.gelu(x, approximate=True)
def _silu(x):
    return jax.nn.silu(x)
def _sigmoid(x):
    return jax.nn.sigmoid(x)
def _layernorm(x, axis=-1, eps=1e-5):
    m = jnp.mean(x, axis=axis, keepdims=True)
    v = jnp.var(x, axis=axis, keepdims=True)
    return (x - m) / jnp.sqrt(v + eps)
def _scatter_add(tgt, idx, src, axis=0):
    return tgt.at[idx].add(src)
def _segment_sum(src, seg, n):
    return jax.ops.segment_sum(src, seg, n)

kernel_name = 'mk_conv_attn_hybrid_d2_conv_nchw128_a9adb0'

def setup_inputs(seed: int = 0):
    np.random.seed(seed)
    _w = jnp.asarray
    def _rec_inputs():
        import jax
        import jax.numpy as jnp
        _gk = jax.random.key(seed)
        x = -0.0001796 + 1 * jax.random.normal(jax.random.fold_in(_gk, 1), (2, 128, 48, 48), jnp.float32)
        return x
    x = _rec_inputs()
    def _L0_conv_setup():
        import jax, jax.numpy as jnp
        import numpy as np
        B = 2
        DIM = 128
        H = 48
        W = 48
        D2 = DIM // 2
        DSTATE = 64
        DCONV = 4

        def _s6_params(key, d, n, k):
            ks = jax.random.split(key, 4)
            conv_w = jax.random.normal(ks[0], (d, k), dtype=jnp.float32) * 0.2
            conv_b = jnp.zeros((d,), jnp.float32)
            Wd = jax.random.normal(ks[1], (d, d), dtype=jnp.float32) / np.sqrt(d)
            bd = jnp.zeros((d,), jnp.float32)
            WB = jax.random.normal(ks[2], (d, n), dtype=jnp.float32) / np.sqrt(d)
            WC = jax.random.normal(ks[3], (d, n), dtype=jnp.float32) / np.sqrt(d)
            Alog = jnp.log(jnp.broadcast_to(jnp.arange(1, n + 1, dtype=jnp.float32), (d, n)))
            Dp = jnp.ones((d,), jnp.float32)
            return (conv_w, conv_b, Wd, bd, WB, WC, Alog, Dp)

        def _s6(u, conv_w, conv_b, Wd, bd, WB, WC, Alog, Dp):
            b, d, L = u.shape
            K = conv_w.shape[1]
            up = jnp.pad(u, ((0, 0), (0, 0), (K - 1, 0)))
            xc = sum((conv_w[:, k][None, :, None] * up[:, :, k:k + L] for k in range(K)))
            xc = jax.nn.silu(xc + conv_b[None, :, None])
            xt = xc.transpose(0, 2, 1)
            delta = jax.nn.softplus(xt @ Wd + bd)
            Bm = xt @ WB
            Cm = xt @ WC
            A = -jnp.exp(Alog)
            dA = jnp.exp(delta[..., None] * A)
            dBx = (delta * xt)[..., None] * Bm[:, :, None, :]

            def combine(c1, c2):
                a1, b1 = c1
                a2, b2 = c2
                return (a2 * a1, a2 * b1 + b2)
            _, h = jax.lax.associative_scan(combine, (dA, dBx), axis=1)
            y = jnp.einsum('bldn,bln->bld', h, Cm) + Dp * xt
            return y.transpose(0, 2, 1)
        key = jax.random.key(seed)
        ks = jax.random.split(key, 5)
        x = jax.random.normal(ks[0], (B, DIM, H, W), dtype=jnp.float32)
        Wx = jax.random.normal(ks[1], (DIM, DIM), dtype=jnp.float32) / np.sqrt(DIM)
        bx = jnp.zeros((DIM,), jnp.float32)
        Wp = jax.random.normal(ks[2], (DIM, DIM), dtype=jnp.float32) / np.sqrt(DIM)
        bp = jnp.zeros((DIM,), jnp.float32)
        f = _s6_params(ks[3], D2, DSTATE, DCONV)
        r = _s6_params(ks[4], D2, DSTATE, DCONV)
        d = {'x': x, 'Wx': Wx, 'bx': bx, 'Wp': Wp, 'bp': bp}
        fn = ['f_conv_w', 'f_conv_b', 'f_Wd', 'f_bd', 'f_WB', 'f_WC', 'f_Alog', 'f_D']
        rn = ['r_conv_w', 'r_conv_b', 'r_Wd', 'r_bd', 'r_WB', 'r_WC', 'r_Alog', 'r_D']
        d.update(dict(zip(fn, f)))
        d.update(dict(zip(rn, r)))
        return d
    _L0_conv_all = _L0_conv_setup()
    _L0_conv_in = {k: v for k, v in _L0_conv_all.items() if k in ('Wx', 'bx', 'Wp', 'bp', 'f_conv_w', 'f_conv_b', 'f_Wd', 'f_bd', 'f_WB', 'f_WC', 'f_Alog', 'f_D', 'r_conv_w', 'r_conv_b', 'r_Wd', 'r_bd', 'r_WB', 'r_WC', 'r_Alog', 'r_D', )}
    del _L0_conv_all

    def _L1_attn_setup():
        import jax, jax.numpy as jnp
        import numpy as np
        DIM = 128
        N_HEADS = 8
        key = jax.random.key(seed)
        k1, k2, k3 = jax.random.split(key, 3)
        B, N = (8, 1024)
        inner = DIM * N_HEADS
        x = jax.random.normal(k1, (B, N, DIM), dtype=jnp.float32)
        w_qkv = jax.random.normal(k2, (DIM, inner * 3), dtype=jnp.float32) * DIM ** (-0.5)
        w_out = jax.random.normal(k3, (inner, DIM), dtype=jnp.float32) * inner ** (-0.5)
        b_out = jnp.zeros((DIM,), dtype=jnp.float32)
        return {'x': x, 'w_qkv': w_qkv, 'w_out': w_out, 'b_out': b_out}
    _L1_attn_all = _L1_attn_setup()
    _L1_attn_in = {k: v for k, v in _L1_attn_all.items() if k in ('w_qkv', 'w_out', 'b_out', )}
    del _L1_attn_all

    def _L1_ffn_setup():
        import jax, jax.numpy as jnp
        import numpy as np
        B, N, D, C, E, K = (8, 8192, 128, 128, 8, 2)
        key = jax.random.key(seed)
        k0, k1, k2 = jax.random.split(key, 3)
        x = jax.random.normal(k0, (B, N, D), dtype=jnp.float32)
        router_w = jax.random.normal(k1, (D, E), dtype=jnp.float32) * 0.05
        router_b = jnp.zeros((E,), dtype=jnp.float32)
        expert_w = jax.random.normal(k2, (E, D, C), dtype=jnp.float32) * (1.0 / np.sqrt(D))
        expert_b = jnp.zeros((E, C), dtype=jnp.float32)
        return {'x': x, 'router_w': router_w, 'router_b': router_b, 'expert_w': expert_w, 'expert_b': expert_b}
    _L1_ffn_all = _L1_ffn_setup()
    _L1_ffn_in = {k: v for k, v in _L1_ffn_all.items() if k in ('router_w', 'router_b', 'expert_w', 'expert_b', )}
    del _L1_ffn_all

    return {
        "x": x,
        "L0_conv_Wx": _L0_conv_in["Wx"],
        "L0_conv_bx": _L0_conv_in["bx"],
        "L0_conv_Wp": _L0_conv_in["Wp"],
        "L0_conv_bp": _L0_conv_in["bp"],
        "L0_conv_f_conv_w": _L0_conv_in["f_conv_w"],
        "L0_conv_f_conv_b": _L0_conv_in["f_conv_b"],
        "L0_conv_f_Wd": _L0_conv_in["f_Wd"],
        "L0_conv_f_bd": _L0_conv_in["f_bd"],
        "L0_conv_f_WB": _L0_conv_in["f_WB"],
        "L0_conv_f_WC": _L0_conv_in["f_WC"],
        "L0_conv_f_Alog": _L0_conv_in["f_Alog"],
        "L0_conv_f_D": _L0_conv_in["f_D"],
        "L0_conv_r_conv_w": _L0_conv_in["r_conv_w"],
        "L0_conv_r_conv_b": _L0_conv_in["r_conv_b"],
        "L0_conv_r_Wd": _L0_conv_in["r_Wd"],
        "L0_conv_r_bd": _L0_conv_in["r_bd"],
        "L0_conv_r_WB": _L0_conv_in["r_WB"],
        "L0_conv_r_WC": _L0_conv_in["r_WC"],
        "L0_conv_r_Alog": _L0_conv_in["r_Alog"],
        "L0_conv_r_D": _L0_conv_in["r_D"],
        "L1_attn_w_qkv": _L1_attn_in["w_qkv"],
        "L1_attn_w_out": _L1_attn_in["w_out"],
        "L1_attn_b_out": _L1_attn_in["b_out"],
        "L1_ffn_router_w": _L1_ffn_in["router_w"],
        "L1_ffn_router_b": _L1_ffn_in["router_b"],
        "L1_ffn_expert_w": _L1_ffn_in["expert_w"],
        "L1_ffn_expert_b": _L1_ffn_in["expert_b"],
    }

def reference(x, L0_conv_Wx, L0_conv_bx, L0_conv_Wp, L0_conv_bp, L0_conv_f_conv_w, L0_conv_f_conv_b, L0_conv_f_Wd, L0_conv_f_bd, L0_conv_f_WB, L0_conv_f_WC, L0_conv_f_Alog, L0_conv_f_D, L0_conv_r_conv_w, L0_conv_r_conv_b, L0_conv_r_Wd, L0_conv_r_bd, L0_conv_r_WB, L0_conv_r_WC, L0_conv_r_Alog, L0_conv_r_D, L1_attn_w_qkv, L1_attn_w_out, L1_attn_b_out, L1_ffn_router_w, L1_ffn_router_b, L1_ffn_expert_w, L1_ffn_expert_b):
    import jax
    import jax.numpy as jnp
    def _L0_conv_ref(x, Wx, bx, Wp, bp, f_conv_w, f_conv_b, f_Wd, f_bd, f_WB, f_WC, f_Alog, f_D, r_conv_w, r_conv_b, r_Wd, r_bd, r_WB, r_WC, r_Alog, r_D):
        import jax, jax.numpy as jnp
        import numpy as np
        B = 2
        DIM = 128
        H = 48
        W = 48
        D2 = DIM // 2
        DSTATE = 64
        DCONV = 4

        def _s6_params(key, d, n, k):
            ks = jax.random.split(key, 4)
            conv_w = jax.random.normal(ks[0], (d, k), dtype=jnp.float32) * 0.2
            conv_b = jnp.zeros((d,), jnp.float32)
            Wd = jax.random.normal(ks[1], (d, d), dtype=jnp.float32) / np.sqrt(d)
            bd = jnp.zeros((d,), jnp.float32)
            WB = jax.random.normal(ks[2], (d, n), dtype=jnp.float32) / np.sqrt(d)
            WC = jax.random.normal(ks[3], (d, n), dtype=jnp.float32) / np.sqrt(d)
            Alog = jnp.log(jnp.broadcast_to(jnp.arange(1, n + 1, dtype=jnp.float32), (d, n)))
            Dp = jnp.ones((d,), jnp.float32)
            return (conv_w, conv_b, Wd, bd, WB, WC, Alog, Dp)

        def _s6(u, conv_w, conv_b, Wd, bd, WB, WC, Alog, Dp):
            b, d, L = u.shape
            K = conv_w.shape[1]
            up = jnp.pad(u, ((0, 0), (0, 0), (K - 1, 0)))
            xc = sum((conv_w[:, k][None, :, None] * up[:, :, k:k + L] for k in range(K)))
            xc = jax.nn.silu(xc + conv_b[None, :, None])
            xt = xc.transpose(0, 2, 1)
            delta = jax.nn.softplus(xt @ Wd + bd)
            Bm = xt @ WB
            Cm = xt @ WC
            A = -jnp.exp(Alog)
            dA = jnp.exp(delta[..., None] * A)
            dBx = (delta * xt)[..., None] * Bm[:, :, None, :]

            def combine(c1, c2):
                a1, b1 = c1
                a2, b2 = c2
                return (a2 * a1, a2 * b1 + b2)
            _, h = jax.lax.associative_scan(combine, (dA, dBx), axis=1)
            y = jnp.einsum('bldn,bln->bld', h, Cm) + Dp * xt
            return y.transpose(0, 2, 1)
        n, c, h, w = x.shape
        t = jnp.einsum('oc,bchw->bohw', Wx, x) + bx[None, :, None, None]
        seq = t.reshape(n, c, h * w)
        half = c // 2
        xF = seq[:, :half]
        xR = jnp.flip(seq[:, half:], axis=-1)
        yF = _s6(xF, f_conv_w, f_conv_b, f_Wd, f_bd, f_WB, f_WC, f_Alog, f_D)
        yR = jnp.flip(_s6(xR, r_conv_w, r_conv_b, r_Wd, r_bd, r_WB, r_WC, r_Alog, r_D), axis=-1)
        y = jnp.concatenate([yF, yR], axis=1).reshape(n, c, h, w)
        return jnp.einsum('oc,bchw->bohw', Wp, y) + bp[None, :, None, None]

    def _L1_attn_ref(x, w_qkv, w_out, b_out):
        import jax, jax.numpy as jnp
        import numpy as np
        DIM = 128
        N_HEADS = 8
        B, N, _ = x.shape
        h, d = (N_HEADS, DIM)
        qkv = x @ w_qkv
        q, k, v = jnp.split(qkv, 3, axis=-1)
        to_heads = lambda t: t.reshape(B, N, h, d).transpose(0, 2, 1, 3)
        q, k, v = (to_heads(q), to_heads(k), to_heads(v))
        scores = jnp.einsum('bhid,bhjd->bhij', q, k) * d ** (-0.5)
        A = jax.nn.softmax(scores, axis=-1)
        z = jnp.einsum('bhij,bhjd->bhid', A, v)
        z = z.transpose(0, 2, 1, 3).reshape(B, N, h * d)
        return z @ w_out + b_out

    def _L1_ffn_ref(x, router_w, router_b, expert_w, expert_b):
        import jax, jax.numpy as jnp
        import numpy as np
        B, N, D, C, E, K = (8, 8192, 128, 128, 8, 2)
        router_probs = jax.nn.softmax(x @ router_w + router_b, axis=-1)
        top_p, top_i = jax.lax.top_k(router_probs, K)
        top_p = top_p / jnp.sum(top_p, axis=-1, keepdims=True)
        expert_out = jnp.einsum('bnd,edc->bnec', x, expert_w) + expert_b
        gathered = jnp.take_along_axis(expert_out, top_i[..., None], axis=2)
        return jnp.einsum('bnk,bnkc->bnc', top_p, gathered)

    def _gn(v, G=32, eps=1e-5):
        B_, C_, H_, W_ = v.shape
        g = v.reshape(B_, G, C_ // G, H_, W_)
        m = jnp.mean(g, axis=(2, 3, 4), keepdims=True)
        s = jnp.var(g, axis=(2, 3, 4), keepdims=True)
        return ((g - m) / jnp.sqrt(s + eps)).reshape(v.shape)

    def _ln_c(v, eps=1e-6):
        m = jnp.mean(v, axis=1, keepdims=True)
        s = jnp.var(v, axis=1, keepdims=True)
        return (v - m) / jnp.sqrt(s + eps)

    def _ln_t(v, eps=1e-5):
        m = jnp.mean(v, axis=-1, keepdims=True)
        s = jnp.var(v, axis=-1, keepdims=True)
        return (v - m) / jnp.sqrt(s + eps)

    def _to_tokens(v):
        B_, C_, H_, W_ = v.shape
        return v.reshape(B_, C_, H_ * W_).transpose(0, 2, 1)
    def _from_tokens(t, like):
        B_, C_, H_, W_ = like.shape
        return t.transpose(0, 2, 1).reshape(B_, C_, H_, W_)

    x = x + _L0_conv_ref(_gn(x), L0_conv_Wx, L0_conv_bx, L0_conv_Wp, L0_conv_bp, L0_conv_f_conv_w, L0_conv_f_conv_b, L0_conv_f_Wd, L0_conv_f_bd, L0_conv_f_WB, L0_conv_f_WC, L0_conv_f_Alog, L0_conv_f_D, L0_conv_r_conv_w, L0_conv_r_conv_b, L0_conv_r_Wd, L0_conv_r_bd, L0_conv_r_WB, L0_conv_r_WC, L0_conv_r_Alog, L0_conv_r_D)
    t = _to_tokens(x)
    t = t + _L1_attn_ref(_ln_t(t), L1_attn_w_qkv, L1_attn_w_out, L1_attn_b_out)
    t = t + _L1_ffn_ref(_ln_t(t), L1_ffn_router_w, L1_ffn_router_b, L1_ffn_expert_w, L1_ffn_expert_b)
    x = _from_tokens(t, x)
    return x


_drawn_inputs = setup_inputs


def setup_inputs(seed=0):
    import zlib

    import numpy as np

    out = dict(_drawn_inputs(seed))
    spreads = {'L0_conv_bx': (0.0, 0.1),
     'L0_conv_bp': (0.0, 0.1),
     'L0_conv_f_conv_b': (0.0, 0.1),
     'L0_conv_f_bd': (0.0, 0.304),
     'L0_conv_f_D': (1.0, 0.2),
     'L0_conv_r_conv_b': (0.0, 0.1),
     'L0_conv_r_bd': (0.0, 0.382),
     'L0_conv_r_D': (1.0, 0.2),
     'L1_attn_b_out': (0.0, 0.1),
     'L1_ffn_router_b': (0.0, 0.1),
     'L1_ffn_expert_b': (0.0, 0.1)}
    factors = {}
    for name, (base, spread) in spreads.items():
        noise = np.random.default_rng([zlib.crc32(name.encode()), seed]).standard_normal(out[name].shape)
        drawn = base * np.exp(spread * noise) if base else spread * noise
        out[name] = jnp.asarray(drawn.astype(out[name].dtype))
    for name, factor in factors.items():
        out[name] = (out[name] * factor).astype(out[name].dtype)
    return out
```

```python
from contextlib import ExitStack

import concourse.bass as bass
from concourse import mybir

ALU = mybir.AluOpType
ACT = mybir.ActivationFunctionType
AX = mybir.AxisListType
F32 = mybir.dt.float32
F16 = mybir.dt.float16
BF16 = mybir.dt.bfloat16
ds = bass.ds

P = 128
NB = 2
L = 48 * 48
NT = L // P
TT = NB * NT
W = 384
NC = L // W
D2 = P // 2
NS = 64
TAPS = 4
NG = 4
GS = NS // NG
NPAIR = NS // 2
NH = 4
H = 8
E = 8
SCALE = float(P) ** -0.5
BANK = 512


class Mem:

    def __init__(self, nc, ctx):
        self.nc, self.ctx = nc, ctx

    def sb(self, name, shape, dt=F32):
        return self.ctx.enter_context(self.nc.sbuf_tensor(name, shape, dt))

    def ps(self, name, shape, dt=F32):
        return self.ctx.enter_context(self.nc.psum_tensor(name, shape, dt))

    def sem(self, name):
        return self.ctx.enter_context(self.nc.semaphore(name))


def load_phase(nc, m, dram, sbuf):
    loaded = m.sem("loaded")
    n = len(sbuf)
    with nc.Block() as block:
        @block.sync
        def _(sp):
            for name in sbuf:
                sp.dma_start(sbuf[name][:], dram[name]).then_inc(loaded, 16)
            sp.wait_ge(loaded, 16 * n)


def stem_phase(nc, m, s):
    xin, u, xt, delta, dx = s["xin"], s["u"], s["xt"], s["delta"], s["dx"]
    par, ident = s["par"], s["ident"]
    bx, cb, bd, dd = (par[:, k:k + 1] for k in (0, 1, 2, 3))
    taps = [par[:, 4 + k:5 + k] for k in range(TAPS)]
    xg = delta
    stats = m.sb("gn_stats", [P, NB, NC, 6])
    mv = m.sb("gn_mv", [P, NB, 2])
    moments = m.sb("gn_moments", [P, NB, 2])
    group = m.sb("gn_group", [P, NB, 2])
    gvar = m.sb("gn_var", [P, NB])
    rstd = m.sb("gn_rstd", [P, NB])
    eps = m.sb("gn_eps", [P, 1])
    gps = m.ps("gn_ps", [P, BANK])
    proj = m.ps("proj_ps", [P, 4, BANK])
    dve = m.sem("stem_dve")
    stats_in = m.sem("moments_ready")
    group_ps = m.sem("group_ready")
    var_in = m.sem("gvar_ready")
    std_in = m.sem("gstd_ready")
    xg_in = m.sem("xg_ready")
    u_ps = m.sem("u_ps_ready")
    u_in = m.sem("u_ready")
    v_in = m.sem("conv_ready")
    xt_in = m.sem("xt_ready")
    z_ps = m.sem("z_ps_ready")
    z_abs = m.sem("z_abs_ready")
    z_used = m.sem("z_ps_used")
    z_exp = m.sem("z_exp_ready")
    u1_in = m.sem("one_plus_exp_ready")
    ln_in = m.sem("ln_ready")
    const_in = m.sem("stem_const")
    with nc.Block() as block:
        @block.vector
        def _(v):
            count = 0

            def link(ins):
                nonlocal count
                count += 1
                ins.then_inc(dve, 1)
                v.wait_ge(dve, count)

            nc.vector.memset(eps[:], 1e-5).then_inc(const_in, 1)
            nc.vector.memset(u[:, :, 0:TAPS - 1], 0.0)
            nc.vector.memset(s["state"][:], 0.0)
            for b in range(NB):
                for c in range(NC):
                    last = nc.vector.bn_stats(stats[:, b, c, :], xin[:, b, c * W:(c + 1) * W])
            link(last)
            for b in range(NB):
                last = nc.vector.bn_aggr(mv[:, b, :], stats[:, b, :, :])
            link(last)
            nc.vector.tensor_copy(moments[:, :, 0], mv[:, :, 0])
            link(nc.vector.tensor_tensor(moments[:, :, 1], mv[:, :, 0], mv[:, :, 0], ALU.mult))
            nc.vector.tensor_tensor(moments[:, :, 1], moments[:, :, 1], mv[:, :, 1],
                                    ALU.add).then_inc(stats_in, 1)
            v.wait_ge(group_ps, 1)
            link(nc.vector.tensor_copy(group[:], gps[:, 0:2 * NB].rearrange("p (b k) -> p b k", b=NB)))
            link(nc.vector.tensor_tensor(gvar[:], group[:, :, 0], group[:, :, 0], ALU.mult))
            nc.vector.tensor_tensor(gvar[:], group[:, :, 1], gvar[:], ALU.subtract).then_inc(var_in, 1)
            v.wait_ge(std_in, 1)
            link(nc.vector.reciprocal(rstd[:], gvar[:]))
            for b in range(NB):
                nc.vector.tensor_scalar(xg[:, b, :], xin[:, b, :], group[:, b, 0:1], rstd[:, b:b + 1],
                                        ALU.subtract, ALU.mult).then_inc(xg_in, 1)
            for b in range(NB):
                v.wait_ge(u_in, 2 * NC * (b + 1))
                link(nc.vector.tensor_scalar(xt[:, b, :], u[:, b, 0:L], taps[0], cb, ALU.mult, ALU.add))
                for k in range(1, TAPS):
                    ins = nc.vector.scalar_tensor_tensor(out=xt[:, b, :], in0=u[:, b, k:k + L], scalar=taps[k],
                                                         in1=xt[:, b, :], op0=ALU.mult, op1=ALU.add)
                    if k < TAPS - 1:
                        link(ins)
                ins.then_inc(v_in, 1)
            for b in range(NB):
                v.wait_ge(z_exp, b + 1)
                scr = s["scratch"][:, b, :]
                link(nc.vector.tensor_scalar(scr, dx[:, b, :], 1.0, None, ALU.add))
                nc.vector.scalar_tensor_tensor(out=dx[:, b, :], in0=scr, scalar=1.0, in1=dx[:, b, :],
                                               op0=ALU.subtract, op1=ALU.subtract).then_inc(u1_in, 1)
                v.wait_ge(u1_in, b + 1)
                link(nc.vector.tensor_tensor(delta[:, b, :], delta[:, b, :], dx[:, b, :], ALU.subtract))
                v.wait_ge(ln_in, b + 1)
                link(nc.vector.tensor_tensor(delta[:, b, :], delta[:, b, :], scr, ALU.add))
                link(nc.vector.tensor_tensor(dx[:, b, :], delta[:, b, :], xt[:, b, :], ALU.mult))

        @block.tensor
        def _(pe):
            pe.wait_ge(stats_in, 1)
            nc.tensor.matmul(gps[:, 0:2 * NB], s["gavg"][:], moments[:].rearrange("p b k -> p (b k)"),
                             start=True, stop=True).then_inc(group_ps, 1)
            for b in range(NB):
                pe.wait_ge(xg_in, b + 1)
                for c in range(NC):
                    k = b * NC + c
                    if k >= 4:
                        pe.wait_ge(u_in, 2 * (k - 3))
                    nc.tensor.matmul(proj[:, k % 4, 0:W], s["wxT"][:], xg[:, b, c * W:(c + 1) * W],
                                     start=True, stop=True).then_inc(u_ps, 1)
            for b in range(NB):
                pe.wait_ge(xt_in, b + 1)
                for c in range(NC):
                    k = b * NC + c
                    if k < 4:
                        pe.wait_ge(u_in, 2 * NB * NC)
                    else:
                        pe.wait_ge(z_used, k - 3)
                    nc.tensor.matmul(proj[:, k % 4, 0:W], s["wd"][:], xt[:, b, c * W:(c + 1) * W],
                                     start=True, stop=True).then_inc(z_ps, 1)

        @block.scalar
        def _(act):
            act.wait_ge(const_in, 1)
            act.wait_ge(var_in, 1)
            nc.scalar.activation(gvar[:], gvar[:], ACT.Sqrt, bias=eps[:]).then_inc(std_in, 1)
            for b in range(NB):
                for c in range(NC):
                    k = b * NC + c
                    act.wait_ge(u_ps, k + 1)
                    lo = TAPS - 1 + c * W
                    nc.scalar.activation(u[0:D2, b, lo:lo + W], proj[0:D2, k % 4, 0:W], ACT.Identity,
                                         bias=bx[0:D2]).then_inc(u_in, 1)
                    hi = TAPS - 1 + L - 1 - c * W
                    nc.scalar.activation(u[D2:P, b, hi - W + 1:hi + 1][:, ::-1], proj[D2:P, k % 4, 0:W],
                                         ACT.Identity, bias=bx[D2:P]).then_inc(u_in, 1)
            for b in range(NB):
                act.wait_ge(v_in, b + 1)
                nc.scalar.activation(xt[:, b, :], xt[:, b, :], ACT.Silu).then_inc(xt_in, 1)
            for b in range(NB):
                act.wait_ge(xt_in, b + 1)
                for c in range(NC):
                    k = b * NC + c
                    act.wait_ge(z_ps, k + 1)
                    cols = slice(c * W, (c + 1) * W)
                    nc.scalar.activation(dx[:, b, cols], proj[:, k % 4, 0:W], ACT.Abs,
                                         bias=bd).then_inc(z_abs, 1)
                    nc.scalar.activation(delta[:, b, cols], proj[:, k % 4, 0:W], ACT.Relu,
                                         bias=bd).then_inc(z_used, 1)
                act.wait_ge(z_abs, NC * (b + 1))
                nc.scalar.activation(dx[:, b, :], dx[:, b, :], ACT.Exp, scale=-1.0).then_inc(z_exp, 1)
            for b in range(NB):
                act.wait_ge(u1_in, b + 1)
                nc.scalar.activation(s["scratch"][:, b, :], s["scratch"][:, b, :], ACT.Ln).then_inc(ln_in, 1)
            nc.scalar.activation(s["alog"][:], s["alog"][:], ACT.Exp).then_inc(const_in, 1)
            act.wait_ge(const_in, 2)
            nc.scalar.mul(s["aneg"][:], s["alog"][:], -1.0)

        @block.gpsimd
        def _(pool):
            nc.gpsimd.tensor_scalar(s["dd"][:], ident[:], dd, None, ALU.mult)
            nc.gpsimd.tensor_copy(s["sel"][:], s["sel32"][:])


def split_phase(nc, m, s, b):
    xt, parts = s["xt"], s["parts"]
    ps = m.ps(f"bc_ps{b}", [P, 4, 2, BANK])
    rest = m.sb(f"bc_rest{b}", [P, 4, 2, W])
    ps_ready = m.sem(f"bc_ps_ready{b}")
    first = m.sem(f"first_part{b}")
    rest_in = m.sem(f"rest_ready{b}")
    second = m.sem(f"second_part{b}")
    third = m.sem(f"third_part{b}")
    jobs = [(g, c) for g in range(2 * NG) for c in range(0, NC, 2)]

    def out(g, c, rows):
        return parts[rows, g, c * W:(c + 2) * W].rearrange("p (j w) -> p j w", j=2)

    with nc.Block() as block:
        @block.tensor
        def _(pe):
            for k, (g, c) in enumerate(jobs):
                if k >= 4:
                    pe.wait_ge(rest_in, k - 3)
                for j in range(2):
                    mm = nc.tensor.matmul(ps[:, k % 4, j, 0:W], s["bcw"][:, g, :],
                                          xt[:, b, (c + j) * W:(c + j + 1) * W], start=True, stop=True)
                mm.then_inc(ps_ready, 1)

        @block.scalar
        def _(act):
            for k, (g, c) in enumerate(jobs):
                act.wait_ge(ps_ready, k + 1)
                nc.scalar.copy(out(g, c, slice(0, P)), ps[:, k % 4, :, 0:W]).then_inc(first, 1)
                if k >= 1:
                    g1, c1 = jobs[k - 1]
                    act.wait_ge(rest_in, k)
                    nc.scalar.copy(out(g1, c1, slice(D2, P)), rest[D2:P, (k - 1) % 4]).then_inc(second, 1)
            act.wait_ge(rest_in, len(jobs))
            nc.scalar.copy(out(*jobs[-1], slice(D2, P)), rest[D2:P, (len(jobs) - 1) % 4]).then_inc(second, 1)

        @block.vector
        def _(v):
            for k, (g, c) in enumerate(jobs):
                v.wait_ge(first, k + 1)
                if k >= 4:
                    v.wait_ge(third, k - 3)
                nc.vector.tensor_tensor(rest[D2:P, k % 4], ps[D2:P, k % 4, :, 0:W], out(g, c, slice(D2, P)),
                                        ALU.subtract).then_inc(rest_in, 1)

        @block.gpsimd
        def _(pool):
            rows = slice(96, P)
            for k, (g, c) in enumerate(jobs):
                pool.wait_ge(second, k + 1)
                nc.gpsimd.tensor_tensor(out(g, c, rows), rest[rows, k % 4], out(g, c, rows),
                                        ALU.subtract).then_inc(third, 1)


def scan_phase(nc, m, s, b):
    xt, delta, dx, u = s["xt"], s["delta"], s["dx"], s["u"]
    parts, sel, aneg, state = s["parts"], s["sel"], s["aneg"], s["state"]
    bps = m.ps(f"b_ps{b}", [P, 2, BANK])
    cps = m.ps(f"c_ps{b}", [P, 2, BANK])
    da = m.ps(f"da_ps{b}", [P, 2, BANK])
    yps = m.ps(f"y_ps{b}", [P, BANK])
    dbx = m.sb(f"dbx{b}", [P, 2, 2, W])
    hh = m.sb(f"h{b}", [P, NH, 2, W])
    csb = m.sb(f"c_sb{b}", [P, NH, 2, W])
    prod = m.sb(f"ch{b}", [P, 2, 2, W])
    names = ("b_ready", "c_ready", "c_copied", "da_ready", "dbx_ready", "scanned", "prod_ready",
             "state_saved", "summed", "y_taken")
    (b_ready, c_ready, c_copied, da_ready, dbx_ready, scanned, prod_ready,
     state_saved, summed, y_taken) = (m.sem(f"{n}{b}") for n in names)
    last_pair = NC * NPAIR - 1

    def pairs(engine, step):
        for c in range(NC):
            head = 1 if c else 1 + NH
            for q in range(head):
                step(c, q, q % NH, c * NPAIR + q)
            with engine.Fori(head // NH, NPAIR // NH - 1) as k:
                for i in range(1, NH + 1):
                    step(c, NH * k + i, i % NH, c * NPAIR + NH * k + i)
            for q in range(NPAIR - NH + 1, NPAIR):
                step(c, q, q % NH, c * NPAIR + q)

    with nc.Block() as block:
        @block.tensor
        def _(pe):
            def broadcast(c, q, n, base, ps, used, ready):
                if not (isinstance(n, int) and n < 1):
                    pe.wait_ge(used, n)
                if isinstance(q, int):
                    c, q = (c + 1, q - NPAIR) if q >= NPAIR else (c, q)
                    g, i = q // (GS // 2), q % (GS // 2)
                    rhs = parts[:, base + g, c * W:(c + 1) * W]
                    lhs = [sel[:, (2 * i + j) * P:(2 * i + j + 1) * P] for j in range(2)]
                else:
                    g, i = q // (GS // 2), q % (GS // 2)
                    flat = parts[:].rearrange("p g l -> p (g l)")
                    rhs = flat[:, ds(g * L + (base * L + c * W), W)]
                    lhs = [sel[:, ds(i * (2 * P) + j * P, P)] for j in range(2)]
                for j in range(2):
                    mm = nc.tensor.matmul(ps[:, j, 0:W], lhs[j], rhs, start=True, stop=True)
                mm.then_inc(ready, 1)

            def broadcast_b(c, q, n):
                if not (isinstance(n, int) and n > last_pair):
                    broadcast(c, q, n, 0, bps, dbx_ready, b_ready)

            def broadcast_c(c, q, n):
                if not (isinstance(n, int) and n > last_pair):
                    broadcast(c, q, n, NG, cps, c_copied, c_ready)

            def add(par, n, closes=False):
                pe.wait_ge(prod_ready, n + 1)
                for j in range(2):
                    mm = nc.tensor.matmul(yps[:, 0:W], s["ident"][:], prod[:, par, j, :],
                                          start=False, stop=closes and j == 1)
                mm.then_inc(summed, 1)

            def step(c, q, buf, n):
                first = isinstance(q, int) and q == 0
                par = buf % 2
                if first and c >= 1:
                    add(1 - par, n - 1, closes=True)
                broadcast_b(c, q + 2, n + 2)
                broadcast_c(c, q + 2, n + 2)
                if first:
                    if c >= 1:
                        pe.wait_ge(y_taken, 2 * c)
                    nc.tensor.matmul(yps[:, 0:W], s["dd"][:], xt[:, b, c * W:(c + 1) * W],
                                     start=True, stop=False)
                else:
                    add(1 - par, n - 1)

            broadcast_b(0, 0, 0)
            broadcast_c(0, 0, 0)
            broadcast_b(0, 1, 1)
            broadcast_c(0, 1, 1)
            pairs(pe, step)
            add(1, last_pair, closes=True)

        @block.scalar
        def _(act):
            def take_y(c):
                act.wait_ge(summed, (c + 1) * NPAIR)
                lo, hi = TAPS - 1 + c * W, TAPS - 1 + L - 1 - c * W
                nc.scalar.copy(u[0:D2, b, lo:lo + W], yps[0:D2, 0:W]).then_inc(y_taken, 1)
                nc.scalar.copy(u[D2:P, b, hi - W + 1:hi + 1][:, ::-1], yps[D2:P, 0:W]).then_inc(y_taken, 1)

            def step(c, q, buf, n):
                early = isinstance(n, int) and n < 1
                for j in range(2):
                    if not early:
                        act.wait_ge(scanned, 2 * n - 1 + j)
                    nc.scalar.activation(da[:, j, 0:W], delta[:, b, c * W:(c + 1) * W], ACT.Exp,
                                         scale=aneg[:, 2 * q + j:2 * q + j + 1] if isinstance(q, int)
                                         else aneg[:, ds(2 * q + j, 1)]).then_inc(da_ready, 1)
                    if j == 0:
                        act.wait_ge(c_ready, n + 1)
                        if not (isinstance(n, int) and n < NH):
                            act.wait_ge(prod_ready, n - NH + 1)
                        nc.scalar.copy(csb[:, buf], cps[:, :, 0:W]).then_inc(c_copied, 1)
                if c >= 1 and isinstance(q, int) and q == 0:
                    take_y(c - 1)

            pairs(act, step)
            take_y(NC - 1)

        @block.vector
        def _(v):
            def times_b(c, par, n):
                v.wait_ge(b_ready, n + 1)
                dxc = dx[:, b, c * W:(c + 1) * W].rearrange("p (o w) -> p o w", o=1).broadcast_to([P, 2, W])
                nc.vector.tensor_tensor(dbx[:, par], bps[:, :, 0:W], dxc, ALU.mult).then_inc(dbx_ready, 1)

            def step(c, q, buf, n):
                par = buf % 2
                if not (isinstance(n, int) and n < NH):
                    v.wait_ge(state_saved, n - NH + 1)
                v.wait_ge(dbx_ready, n + 1)
                for j in range(2):
                    v.wait_ge(da_ready, 2 * n + 1 + j)
                    initial = state[:, 2 * q + j:2 * q + j + 1] if isinstance(q, int) else \
                        state[:, ds(2 * q + j, 1)]
                    nc.vector.tensor_tensor_scan(hh[:, buf, j, :], da[:, j, 0:W], dbx[:, par, j, :],
                                                 initial if c else 0.0, ALU.mult,
                                                 ALU.add).then_inc(scanned, 1)
                    if j == 0 and not (isinstance(n, int) and n == last_pair):
                        if not (isinstance(n, int) and n < 1):
                            v.wait_ge(scanned, 2 * n)
                        times_b(c + (isinstance(q, int) and q == NPAIR - 1), 1 - par, n + 1)

            times_b(0, 0, 0)
            pairs(v, step)

        @block.gpsimd
        def _(pool):
            def step(c, q, buf, n):
                par = buf % 2
                pool.wait_ge(scanned, 2 * n + 2)
                pool.wait_ge(c_copied, n + 1)
                if not (isinstance(n, int) and n < 2):
                    pool.wait_ge(summed, n - 1)
                nc.gpsimd.tensor_tensor(prod[:, par], hh[:, buf], csb[:, buf], ALU.mult).then_inc(prod_ready, 1)
                keep = state[:, 2 * q:2 * q + 2] if isinstance(q, int) else state[:, ds(2 * q, 2)]
                nc.gpsimd.tensor_copy(keep, hh[:, buf, :, W - 1]).then_inc(state_saved, 1)

            pairs(pool, step)


def token_phase(nc, m, s):
    t, u, xin, ident = s["t"], s["u"], s["xin"], s["ident"]
    tok_hi, tok_lo, xT_hi, xT_lo = s["tok_hi"], s["tok_lo"], s["xT_hi"], s["xT_lo"]
    tps = m.ps("t_ps", [P, 2, 4, P])
    xps = m.ps("xh_ps", [P, 2, 4, P])
    stats = m.sb("ln1_stats", [P, TT, 6])
    mv = m.sb("ln1_mv", [P, TT, 2])
    std = m.sb("ln1_std", [P, TT])
    rstd = m.sb("ln1_rstd", [P, TT])
    eps = m.sb("ln1_eps", [P, 1])
    xh = m.sb("xh", [P, TT, P])
    t_ps = m.sem("t_ps_ready")
    t_in = m.sem("t_ready")
    st = m.sem("ln1_stats_ready")
    mv_in = m.sem("ln1_mv_ready")
    std_in = m.sem("ln1_std_ready")
    rstd_in = m.sem("ln1_rstd_ready")
    xh_in = m.sem("xh_ready")
    ones_in = m.sem("xh_ones")
    hi_in = m.sem("tok_hi_ready")
    x_ps = m.sem("xT_ps_ready")
    xhi = m.sem("xT_hi_ready")
    xlo = m.sem("xT_lo_ready")
    NQ = TT // 4
    with nc.Block() as block:
        @block.tensor
        def _(pe):
            for k in range(NQ):
                if k >= 2:
                    pe.wait_ge(t_in, k - 1)
                for r in range(4):
                    b, i = divmod(4 * k + r, NT)
                    lo = TAPS - 1 + i * P
                    nc.tensor.matmul(tps[:, k % 2, r, :], u[:, b, lo:lo + P], s["wpT"][:],
                                     start=True, stop=False)
                    mm = nc.tensor.matmul(tps[:, k % 2, r, :], xin[:, b, i * P:(i + 1) * P], ident[:],
                                          start=False, stop=True)
                mm.then_inc(t_ps, 1)
            pe.wait_ge(ones_in, 1)
            for k in range(NQ):
                if k >= 2:
                    pe.wait_ge(xlo, k - 1)
                for r in range(4):
                    mm = nc.tensor.transpose(xps[:, k % 2, r, :], xh[:, 4 * k + r, :], ident[:])
                mm.then_inc(x_ps, 1)

        @block.vector
        def _(v):
            nc.vector.memset(eps[:], 1e-5)
            for k in range(NQ):
                v.wait_ge(t_ps, k + 1)
                bp = s["rows"][:, 0:P].rearrange("p (o c) -> p o c", o=1).broadcast_to([P, 4, P])
                nc.vector.tensor_tensor(t[:, 4 * k:4 * k + 4, :], tps[:, k % 2], bp, ALU.add).then_inc(t_in, 1)
            v.wait_ge(t_in, NQ)
            for k in range(TT):
                last = nc.vector.bn_stats(stats[:, k, :], t[:, k, :])
            last.then_inc(st, 1)
            v.wait_ge(st, 1)
            for k in range(TT):
                last = nc.vector.bn_aggr(mv[:, k, :], stats[:, k, :])
            last.then_inc(mv_in, 1)
            v.wait_ge(std_in, 1)
            nc.vector.reciprocal(rstd[:], std[:]).then_inc(rstd_in, 1)
            v.wait_ge(rstd_in, 1)
            for k in range(TT):
                last = nc.vector.tensor_scalar(xh[:, k, :], t[:, k, :], mv[:, k, 0:1], rstd[:, k:k + 1],
                                               ALU.subtract, ALU.mult)
            last.then_inc(xh_in, 1)
            v.wait_ge(xh_in, 1)
            nc.vector.memset(xh[:, :, 0], 1.0).then_inc(ones_in, 1)
            bo = s["rows"][:, P:2 * P].rearrange("p (o c) -> p o c", o=1).broadcast_to([P, TT, P])
            nc.vector.tensor_tensor(t[:], t[:], bo, ALU.add)
            for k in range(NQ):
                v.wait_ge(xhi, k + 1)
                cols = slice(4 * k * P, (4 * k + 4) * P)
                nc.vector.tensor_tensor(xT_lo[:, cols], xps[:, k % 2].rearrange("p r t -> p (r t)"),
                                        xT_hi[:, cols], ALU.subtract).then_inc(xlo, 1)

        @block.scalar
        def _(act):
            act.wait_ge(mv_in, 1)
            nc.scalar.activation(std[:], mv[:, :, 1], ACT.Sqrt, bias=eps[:]).then_inc(std_in, 1)
            for k in range(NQ):
                act.wait_ge(x_ps, k + 1)
                nc.scalar.copy(xT_hi[:, 4 * k * P:(4 * k + 4) * P],
                               xps[:, k % 2].rearrange("p r t -> p (r t)")).then_inc(xhi, 1)

        @block.gpsimd
        def _(pool):
            pool.wait_ge(ones_in, 1)
            nc.gpsimd.tensor_copy(tok_hi[:], xh[:]).then_inc(hi_in, 1)
            pool.wait_ge(hi_in, 1)
            nc.gpsimd.tensor_tensor(tok_lo[:], xh[:], tok_hi[:], ALU.subtract)


def weight_phase(nc, m, s):
    wqkvT, wo = s["wqkvT"], s["wo"]
    m_hi, m_lo, vo, escale = s["m_hi"], s["m_lo"], s["vo"], s["escale"]
    dT = m.sb("w_less_c0", [P, 3, H, P])
    wps = m.ps("w_ps", [P, 4, 4, P])
    ext = m.sb("m_ext", [P, 2, H])
    big = m.sb("m_big", [P, H])
    allbig = m.sb("m_allbig", [P, H])
    inv = m.sb("m_inv", [P, H])
    mn = m.sb("m_norm", [P, H, P])
    d_in = m.sem("w_less_ready")
    w_ps = m.sem("w_ps_ready")
    step_in = m.sem("w_step")
    big_in = m.sem("m_big_ready")
    all_in = m.sem("m_allbig_ready")
    with nc.Block() as block:
        @block.vector
        def _(v):
            count = 0

            def link(ins):
                nonlocal count
                count += 1
                ins.then_inc(step_in, 1)
                v.wait_ge(step_in, count)

            for k in range(3):
                for h in range(H):
                    last = nc.vector.tensor_scalar(dT[:, k, h, :], wqkvT[:, k, h, :], wqkvT[:, k, h, 0:1],
                                                   None, ALU.subtract)
            last.then_inc(d_in, 1)
            nc.vector.memset(vo[:], 0.0)
            v.wait_ge(w_ps, 1)
            qk = wps[:, 0:2].rearrange("p a r e -> p (a r) e")
            nc.vector.tensor_reduce(ext[:, 0, :], qk, AX.X, ALU.max)
            link(nc.vector.tensor_reduce(ext[:, 1, :], qk, AX.X, ALU.min))
            nc.vector.scalar_tensor_tensor(out=big[:], in0=ext[:, 1, :], scalar=-1.0, in1=ext[:, 0, :],
                                           op0=ALU.mult, op1=ALU.max).then_inc(big_in, 1)
            v.wait_ge(all_in, 1)
            link(nc.vector.tensor_scalar(allbig[:], allbig[:], 1e-30, None, ALU.max))
            link(nc.vector.reciprocal(inv[:], allbig[:]))
            nc.vector.tensor_scalar(escale[:], allbig[:], SCALE, None, ALU.mult)
            for h in range(H):
                last = nc.vector.tensor_scalar(mn[:, h, :], wps[:, h // 4, h % 4, :], inv[:, h:h + 1], None,
                                               ALU.mult)
            link(last)
            link(nc.vector.tensor_copy(m_hi[:], mn[:].rearrange("p h e -> p (h e)")))
            nc.vector.tensor_tensor(m_lo[:], mn[:].rearrange("p h e -> p (h e)"), m_hi[:], ALU.subtract)
            v.wait_ge(w_ps, 2)
            nc.vector.tensor_copy(vo[:, :, 0:P], wps[:, 2:4].rearrange("p a r e -> p (a r) e"))
            nc.vector.memset(vo[0:1, :, P:P + 1], 1.0)
            nc.vector.tensor_copy(s["ident16"][:], s["ident"][:])

        @block.tensor
        def _(pe):
            pe.wait_ge(d_in, 1)
            for h in range(H):
                mm = nc.tensor.matmul(wps[:, h // 4, h % 4, :], dT[:, 0, h, :], dT[:, 1, h, :],
                                      start=True, stop=True)
            mm.then_inc(w_ps, 1)
            for h in range(H):
                mm = nc.tensor.matmul(wps[:, 2 + h // 4, h % 4, :], dT[:, 2, h, :], wo[:, h, :],
                                      start=True, stop=True)
            mm.then_inc(w_ps, 1)

        @block.gpsimd
        def _(pool):
            pool.wait_ge(big_in, 1)
            nc.gpsimd.partition_all_reduce(allbig[:], big[:], P, bass.bass_isa.ReduceOp.max).then_inc(all_in, 1)


def attention_phase(nc, m, s):
    t, xT_hi, xT_lo, tok_hi, tok_lo = s["t"], s["xT_hi"], s["xT_lo"], s["tok_hi"], s["tok_lo"]
    m_hi, m_lo, vo, escale, ident16 = s["m_hi"], s["m_lo"], s["vo"], s["escale"], s["ident16"]
    NF = NB * H * NC
    KP = NT // 2
    RING = 8
    TC = W // P
    q_hi = m.sb("q_hi", [P, RING * W], F16)
    q_lo = m.sb("q_lo", [P, RING * W], F16)
    p32 = m.sb("p32", [P, 3, 2, W])
    p_hi = m.sb("p_hi", [P, 3, 2, W], F16)
    p_lo = m.sb("p_lo", [P, 3, 2, W], F16)
    z = m.sb("z", [P, 2, W])
    mxp = m.sb("max_parts", [P, 2, TC, 3])
    mx_sb = m.sb("maximum", [P, 2, TC])
    mneg = m.sb("max_neg", [P, 2, TC], F16)
    rl = m.sb("sum_inv", [P, 2, TC])
    scale = m.sb("head_scale", [P, 2])
    sps = m.ps("s_ps", [P, 2, 2, BANK])
    mps = m.ps("max_ps", [P, 2, BANK])
    pvps = m.ps("pv_ps", [P, BANK])
    misc = m.ps("misc_ps", [P, BANK])
    OW = P + 1
    vo_flat = vo[:].rearrange("p h o -> p (h o)")
    t_flat = t[:].rearrange("p t c -> p (t c)")
    tok_hi, tok_lo = (x[:].rearrange("p t c -> p (t c)") for x in (tok_hi, tok_lo))
    out_ps = misc[:, 0:TC * OW].rearrange("p (t o) -> p t o", t=TC)

    q_ps = m.sem("q_ps_ready")
    qh_in = m.sem("q_hi_ready")
    ql_in = m.sem("q_lo_ready")
    s_ready = m.sem("scores_ready")
    exp_hi = m.sem("exp_hi_ready")
    exp_in = m.sem("exp_ready")
    lo_in = m.sem("p_lo_ready")
    pv_done = m.sem("pv_done")
    z_in = m.sem("z_ready")
    mx_ps = m.sem("max_ps_ready")
    mx_part = m.sem("max_part_ready")
    mx_in = m.sem("max_ready")
    mneg_in = m.sem("max_neg_ready")
    row_ps = m.sem("max_row_ps_ready")
    row_in = m.sem("max_row_ready")
    o_ps = m.sem("out_ps_ready")
    rl_in = m.sem("sum_inv_ready")
    o_in = m.sem("out_added")
    scale_in = m.sem("head_scale_ready")

    def image(F):
        return F // (H * NC)

    def at(F):
        return (F % RING) * W

    def tile(F):
        return image(F) * NT + (F % NC) * TC

    def head(F):
        return (F // NC) % H

    LEAD = 4
    MLEAD = 2

    def schedule(engine, body):
        def turn(G, half, proj=True, mx=True, row=True, main=True, prev=True):
            body(G, half, proj, mx, row, main, prev)

        def turns(first, end, **parts):
            if first < end:
                with engine.Fori(first // 2, end // 2) as k:
                    turn(2 * k, 0, **parts)
                    turn(2 * k + 1, 1, **parts)

        for G in range(2):
            turn(G, G, mx=False, row=False, main=False, prev=False)
        turns(2, MLEAD, mx=False, row=False, main=False, prev=False)
        turn(MLEAD, 0, row=False, main=False, prev=False)
        turn(MLEAD + 1, 1, main=False, prev=False)
        turns(MLEAD + 2, LEAD, main=False, prev=False)
        turn(LEAD, 0, prev=False)
        turn(LEAD + 1, 1)
        turns(LEAD + 2, NF)
        turns(NF, NF + MLEAD, proj=False)
        turn(NF + MLEAD, 0, proj=False, mx=False)
        turn(NF + MLEAD + 1, 1, proj=False, mx=False, row=False)
        turns(NF + MLEAD + 2, NF + LEAD, proj=False, mx=False, row=False)

    def wait(engine, sem, value):
        if not isinstance(value, int) or value > 0:
            engine.wait_ge(sem, value)

    with nc.Block() as block:
        @block.tensor
        def _(pe):
            def misc_free(G, user, proj, row, prev):
                if user == "out" and row:
                    pe.wait_ge(row_in, G - MLEAD)
                elif user != "proj" and proj:
                    pe.wait_ge(qh_in, G + 1)
                    pe.wait_ge(ql_in, G + 1)
                elif prev:
                    wait(pe, o_in, G - LEAD - 1)
                    if isinstance(G, int) and G == LEAD + 1:
                        pe.wait_ge(row_in, G - MLEAD - 1)
                elif row:
                    pe.wait_ge(row_in, G - MLEAD - 1)
                    pe.wait_ge(ql_in, G)
                elif not (isinstance(G, int) and G == 0):
                    pe.wait_ge(qh_in, G)
                    pe.wait_ge(ql_in, G)

            def project(G):
                cols = ds(image(G) * L + (G % NC) * W, W)
                w = ds(head(G) * P, P)
                nc.tensor.matmul(misc[:, 0:W], m_hi[:, w], xT_hi[:, cols], start=True, stop=False)
                nc.tensor.matmul(misc[:, 0:W], m_hi[:, w], xT_lo[:, cols], start=False, stop=False)
                nc.tensor.matmul(misc[:, 0:W], m_lo[:, w], xT_hi[:, cols], start=False,
                                 stop=True).then_inc(q_ps, 1)

            def weighted_sum(kp, F, n):
                if kp == 0:
                    wait(pe, z_in, F)
                wait(pe, lo_in, n + 1)
                k0 = image(F) * NT * P
                for j in range(2):
                    keys = ds(k0 + (2 * kp + j) * P, P)
                    hi, lo = p_hi[:, kp % 3, j, :], p_lo[:, kp % 3, j, :]
                    nc.tensor.matmul(pvps[:, 0:W], tok_hi[:, keys], hi, start=kp + j == 0, stop=False)
                    nc.tensor.matmul(pvps[:, 0:W], tok_hi[:, keys], lo, start=False, stop=False)
                    mm = nc.tensor.matmul(pvps[:, 0:W], tok_lo[:, keys], hi, start=False,
                                          stop=kp == KP - 1 and j == 1)
                mm.then_inc(pv_done, 1)

            def output(F, par):
                pe.wait_ge(z_in, F + 1)
                w = ds(head(F) * OW, OW)
                for i in range(TC):
                    mm = nc.tensor.matmul(out_ps[:, i, :], z[:, par, i * P:(i + 1) * P], vo_flat[:, w],
                                          start=True, stop=True)
                mm.then_inc(o_ps, 1)

            def body(G, half, proj, mx, row, main, prev):
                F, M, R = G - LEAD, G - MLEAD, G - MLEAD - 1
                for kp in range(KP):
                    n, nm = F * KP + kp, M * KP + kp
                    if kp == 0 and proj:
                        misc_free(G, "proj", proj, row, prev)
                        project(G)
                    if kp == 3 and row:
                        misc_free(G, "row", proj, row, prev)
                        pe.wait_ge(mneg_in, R + 1)
                        for i in range(TC):
                            mm = nc.tensor.matmul(misc[0:1, i * P:(i + 1) * P], mneg[:, 1 - half, i:i + 1],
                                                  ident16[:], start=True, stop=True)
                        mm.then_inc(row_ps, 1)
                    if kp == 5 and prev:
                        misc_free(G, "out", proj, row, prev)
                        output(F - 1, 1 - half)
                    if main:
                        if kp == 0:
                            pe.wait_ge(row_in, F + 1)
                        wait(pe, exp_in, n - 1)
                        q = ds(at(F), W)
                        k0 = image(F) * L
                        sb = (half + kp) % 2
                        for j in range(2):
                            keys = ds(k0 + (2 * kp + j) * P, P)
                            o = sps[:, sb, j, 0:W]
                            nc.tensor.matmul(o, xT_hi[:, keys], q_hi[:, q], start=True, stop=False)
                            nc.tensor.matmul(o, xT_hi[:, keys], q_lo[:, q], start=False, stop=False)
                            mm = nc.tensor.matmul(o, xT_lo[:, keys], q_hi[:, q], start=False, stop=True)
                        mm.then_inc(s_ready, 1)
                    if mx:
                        if kp == 0:
                            pe.wait_ge(qh_in, M + 1)
                        wait(pe, mx_part, nm)
                        q = ds(at(M) + (kp // 3) * P, P)
                        for j in range(2):
                            keys = ds(image(M) * L + (2 * (kp % 3) + j) * W, W)
                            mm = nc.tensor.matmul(mps[:, j, 0:W], q_hi[:, q], xT_hi[:, keys],
                                                  start=True, stop=True)
                        mm.then_inc(mx_ps, 1)
                    if kp >= 2 and main:
                        weighted_sum(kp - 2, F, n - 2)
                    elif kp < 2 and prev:
                        weighted_sum(kp + KP - 2, F - 1, n - 2)

            schedule(pe, body)
            for kp in (KP - 2, KP - 1):
                weighted_sum(kp, NF - 1, (NF - 1) * KP + kp)
            pe.wait_ge(o_in, NF - 1)
            output(NF - 1, 1)

        @block.scalar
        def _(act):
            def take_z(F, par):
                act.wait_ge(pv_done, (F + 1) * KP)
                wait(act, o_ps, F)
                nc.scalar.copy(z[:, par, :], pvps[:, 0:W]).then_inc(z_in, 1)

            def body(G, half, proj, mx, row, main, prev):
                F, R = G - LEAD, G - MLEAD - 1
                if main:
                    nc.scalar.copy(scale[:, half:half + 1], escale[:, ds(head(F), 1)]).then_inc(scale_in, 1)
                    act.wait_ge(scale_in, F + 1)
                for kp in range(KP):
                    if kp == 0 and proj:
                        act.wait_ge(q_ps, G + 1)
                        nc.scalar.copy(q_hi[:, ds(at(G), W)], misc[:, 0:W]).then_inc(qh_in, 1)
                    if kp == 2 and prev:
                        take_z(F - 1, 1 - half)
                    if kp == 3 and row:
                        act.wait_ge(row_ps, R + 1)
                        nc.scalar.copy(q_hi[0:1, ds(at(R), W)], misc[0:1, 0:W]).then_inc(row_in, 1)
                    if main:
                        n = F * KP + kp
                        src = sps[:, (half + kp) % 2, :, 0:W]
                        sc = scale[:, half:half + 1]
                        act.wait_ge(s_ready, n + 1)
                        wait(act, pv_done, n - 2)
                        nc.scalar.activation(p_hi[:, kp % 3], src, ACT.Exp, scale=sc).then_inc(exp_hi, 1)
                        wait(act, lo_in, n - 2)
                        nc.scalar.activation(p32[:, kp % 3], src, ACT.Exp, scale=sc).then_inc(exp_in, 1)

            schedule(act, body)
            take_z(NF - 1, 1)

        @block.vector
        def _(v):
            def add_output(F, par):
                v.wait_ge(o_ps, F + 1)
                nc.vector.reciprocal(rl[:, par, :], out_ps[:, :, P]).then_inc(rl_in, 1)
                v.wait_ge(rl_in, F + 1)
                for i in range(TC):
                    tok = t_flat[:, ds((tile(F) + i) * P, P)]
                    ins = nc.vector.scalar_tensor_tensor(out=tok, in0=out_ps[:, i, 0:P],
                                                         scalar=rl[:, par, i:i + 1], in1=tok,
                                                         op0=ALU.mult, op1=ALU.add)
                ins.then_inc(o_in, 1)

            def body(G, half, proj, mx, row, main, prev):
                F, M, R = G - LEAD, G - MLEAD, G - MLEAD - 1
                if row:
                    v.wait_ge(mx_part, (R + 1) * KP)
                    nc.vector.tensor_reduce(mx_sb[:, 1 - half, :], mxp[:, 1 - half], AX.X,
                                            ALU.max).then_inc(mx_in, 1)
                    v.wait_ge(mx_in, R + 1)
                    nc.vector.tensor_scalar(mneg[:, 1 - half, :], mx_sb[:, 1 - half, :], -1.0, None,
                                            ALU.mult).then_inc(mneg_in, 1)
                for kp in range(KP):
                    n, nm = F * KP + kp, M * KP + kp
                    if mx:
                        v.wait_ge(mx_ps, nm + 1)
                        nc.vector.tensor_reduce(mxp[:, half, kp // 3, kp % 3:kp % 3 + 1], mps[:, :, 0:W],
                                                AX.XY, ALU.max).then_inc(mx_part, 1)
                    if kp == 0 and proj:
                        v.wait_ge(qh_in, G + 1)
                        cols = ds(at(G), W)
                        nc.vector.tensor_tensor(q_lo[:, cols], misc[:, 0:W], q_hi[:, cols],
                                                ALU.subtract).then_inc(ql_in, 1)
                    if kp == 5 and prev:
                        add_output(F - 1, 1 - half)
                    if main:
                        v.wait_ge(exp_in, n + 1)
                        wait(v, pv_done, n - 2)
                        nc.vector.tensor_tensor(p_lo[:, kp % 3], p32[:, kp % 3], p_hi[:, kp % 3],
                                                ALU.subtract).then_inc(lo_in, 1)

            schedule(v, body)
            add_output(NF - 1, 1)


def expert_phase(nc, m, s, out):
    t, ident = s["t"], s["ident"]
    stats = m.sb("ln2_stats", [P, TT, 6])
    mv = m.sb("ln2_mv", [P, TT, 2])
    std = m.sb("ln2_std", [P, TT])
    rstd = m.sb("ln2_rstd", [P, TT])
    eps = m.sb("ln2_eps", [P, 1])
    x2 = m.sb("x2", [P, TT, P])
    x2T = m.sb("x2T", [P, TT, P])
    lg = m.sb("logits", [P, TT, E])
    before = m.sb("before", [P, E, E])
    gt = m.sb("greater", [P, TT, E, E])
    eq = m.sb("equal", [P, TT, E, E])
    rank = m.sb("rank", [P, TT, E])
    top = m.sb("top", [P, TT])
    ex = m.sb("router_exp", [P, TT, E])
    den = m.sb("top_sum", [P, TT])
    wgt = m.sb("weight", [P, TT, E])
    wT = m.sb("weightT", [E, TT * P])
    ob = m.sb("out_sb", [P, 2, 4 * P])
    aps = m.ps("a_ps", [P, 2, BANK])
    rps = m.ps("router_ps", [P, BANK])
    eps_ps = m.ps("expert_ps", [P, 2, 2, BANK])
    dve = m.sem("expert_dve")
    mv_in = m.sem("ln2_mv_ready")
    std_in = m.sem("ln2_std_ready")
    x2_in = m.sem("x2_ready")
    a_ps = m.sem("a_ps_ready")
    a_used = m.sem("a_ps_used")
    r_ps = m.sem("router_ps_ready")
    sub_in = m.sem("less_top_ready")
    ex_in = m.sem("router_exp_ready")
    w_in = m.sem("weight_ready")
    e_ps = m.sem("expert_ps_ready")
    e_used = m.sem("expert_added")
    stored = [m.sem(f"stored{j}") for j in range(2)]
    NQ = TT // 4
    with nc.Block() as block:
        @block.vector
        def _(v):
            count = 0

            def link(ins):
                nonlocal count
                count += 1
                ins.then_inc(dve, 1)
                v.wait_ge(dve, count)

            nc.vector.memset(eps[:], 1e-5)
            link(nc.vector.memset(before[:], 0.0))
            for e in range(1, E):
                nc.vector.memset(before[:, e, 0:e], 1.0)
            for k in range(TT):
                last = nc.vector.bn_stats(stats[:, k, :], t[:, k, :])
            link(last)
            for k in range(TT):
                last = nc.vector.bn_aggr(mv[:, k, :], stats[:, k, :])
            last.then_inc(mv_in, 1)
            v.wait_ge(std_in, 1)
            link(nc.vector.reciprocal(rstd[:], std[:]))
            for k in range(TT):
                ins = nc.vector.tensor_scalar(x2[:, k, :], t[:, k, :], mv[:, k, 0:1], rstd[:, k:k + 1],
                                              ALU.subtract, ALU.mult)
                if k % 4 == 3:
                    ins.then_inc(x2_in, 1)
            v.wait_ge(r_ps, 1)
            rb = s["rows"][:, 2 * P:2 * P + E].rearrange("p (o c) -> p o c", o=1).broadcast_to([P, TT, E])
            link(nc.vector.tensor_tensor(lg[:], rps[:, 0:TT * E].rearrange("p (t e) -> p t e", t=TT), rb,
                                         ALU.add))
            link(nc.vector.tensor_reduce(top[:], lg[:], AX.X, ALU.max))
            full = [P, TT, E, E]
            topb = top[:].rearrange("p (t o) -> p t o", o=1).broadcast_to([P, TT, E])
            nc.vector.tensor_tensor(ex[:], lg[:], topb, ALU.subtract).then_inc(sub_in, 1)
            mine = lg[:].rearrange("p t (e o) -> p t e o", o=1).broadcast_to(full)
            other = lg[:].rearrange("p t (o j) -> p t o j", o=1).broadcast_to(full)
            pre = before[:].rearrange("p (o e) j -> p o e j", o=1).broadcast_to(full)
            nc.vector.tensor_tensor(gt[:], other, mine, ALU.is_gt)
            link(nc.vector.tensor_tensor(eq[:], other, mine, ALU.is_equal))
            link(nc.vector.tensor_tensor(eq[:], eq[:], pre, ALU.mult))
            link(nc.vector.tensor_tensor(gt[:], gt[:], eq[:], ALU.add))
            link(nc.vector.tensor_reduce(rank[:], gt[:], AX.X, ALU.add))
            v.wait_ge(ex_in, 1)
            link(nc.vector.scalar_tensor_tensor(out=ex[:], in0=rank[:], scalar=2.0, in1=ex[:],
                                                op0=ALU.is_lt, op1=ALU.mult))
            link(nc.vector.tensor_reduce(den[:], ex[:], AX.X, ALU.add))
            link(nc.vector.reciprocal(den[:], den[:]))
            denb = den[:].rearrange("p (t o) -> p t o", o=1).broadcast_to([P, TT, E])
            nc.vector.tensor_tensor(wgt[:], ex[:], denb, ALU.mult).then_inc(w_in, 1)
            v.wait_ge(w_in, 1)
            for k in range(0, TT, 2):
                for e in range(E):
                    if e % 4 == 0:
                        v.wait_ge(e_ps, k + 1 + e // 4)
                    for r in range(2):
                        if e:
                            v.wait_ge(e_used, k * E + 2 * e + r - 1)
                        nc.vector.scalar_tensor_tensor(
                            out=t[:, k + r, :], in0=eps_ps[:, r, e // 4, (e % 4) * P:(e % 4 + 1) * P],
                            scalar=wgt[:, k + r, e:e + 1], in1=t[:, k + r, :], op0=ALU.mult,
                            op1=ALU.add).then_inc(e_used, 1)

        @block.tensor
        def _(pe):
            for k in range(NQ):
                pe.wait_ge(x2_in, k + 1)
                if k >= 2:
                    pe.wait_ge(a_used, k - 1)
                for r in range(4):
                    mm = nc.tensor.transpose(aps[:, k % 2, r * P:(r + 1) * P], x2[:, 4 * k + r, :], ident[:])
                mm.then_inc(a_ps, 1)
            pe.wait_ge(a_used, NQ)
            for k in range(TT):
                mm = nc.tensor.matmul(rps[:, k * E:(k + 1) * E], x2T[:, k, :], s["rw"][:], start=True,
                                      stop=True)
            mm.then_inc(r_ps, 1)

            def experts(k):
                for j in range(2):
                    if k >= 2:
                        pe.wait_ge(e_used, (k - 2) * E + (j + 1) * E)
                    for r in range(2):
                        mm = nc.tensor.matmul(eps_ps[:, r, j, :], x2T[:, k + r, :],
                                              s["ew"][:, 4 * j:4 * j + 4, :].rearrange("p e c -> p (e c)"),
                                              start=True, stop=True)
                    mm.then_inc(e_ps, 1)

            def result(k):
                pe.wait_ge(a_used, NQ + NQ + k - 1 if k >= 1 else 2 * NQ)
                pe.wait_ge(e_used, (4 * k + 4) * E)
                for r in range(4):
                    i = 4 * k + r
                    o = aps[:, k % 2, r * P:(r + 1) * P]
                    nc.tensor.matmul(o, t[:, i, :], ident[:], start=True, stop=False)
                    mm = nc.tensor.matmul(o, s["eb"][:], wT[:, i * P:(i + 1) * P], start=False, stop=True)
                mm.then_inc(a_ps, 1)

            experts(0)
            pe.wait_ge(w_in, 1)
            for k in range(NQ):
                pe.wait_ge(a_used, NQ + k - 1)
                for r in range(4):
                    mm = nc.tensor.transpose(aps[0:E, k % 2, r * P:(r + 1) * P], wgt[:, 4 * k + r, :],
                                             ident[:])
                mm.then_inc(a_ps, 1)
            for k in range(2, TT, 2):
                experts(k)
                if k % 4 == 0:
                    result(k // 4 - 1)
            result(NQ - 1)

        @block.scalar
        def _(act):
            act.wait_ge(mv_in, 1)
            nc.scalar.activation(std[:], mv[:, :, 1], ACT.Sqrt, bias=eps[:]).then_inc(std_in, 1)
            for k in range(NQ):
                act.wait_ge(a_ps, k + 1)
                nc.scalar.copy(x2T[:, 4 * k:4 * k + 4, :].rearrange("p r t -> p (r t)"),
                               aps[:, k % 2, :]).then_inc(a_used, 1)
            act.wait_ge(sub_in, 1)
            nc.scalar.activation(ex[:], ex[:], ACT.Exp).then_inc(ex_in, 1)
            for k in range(NQ):
                act.wait_ge(a_ps, NQ + k + 1)
                nc.scalar.copy(wT[:, 4 * k * P:(4 * k + 4) * P], aps[0:E, k % 2, :]).then_inc(a_used, 1)
            for k in range(NQ):
                act.wait_ge(a_ps, 2 * NQ + k + 1)
                if k >= 2:
                    act.wait_ge(stored[k % 2], 16 * SPL[k - 2])
                nc.scalar.copy(ob[:, k % 2, :], aps[:, k % 2, :]).then_inc(a_used, 1)

        @block.sync
        def _(sp):
            for k in range(NQ):
                sp.wait_ge(a_used, 2 * NQ + k + 1)
                for b, lo, hi in SPANS[k]:
                    off = lo - 4 * k * P
                    sp.dma_start(out[b, :, lo - b * L:hi - b * L],
                                 ob[:, k % 2, off:off + hi - lo]).then_inc(stored[k % 2], 16)
            for k in (NQ - 2, NQ - 1):
                sp.wait_ge(stored[k % 2], 16 * SPL[k])


def spans(k):
    lo, hi = 4 * k * P, (4 * k + 4) * P
    return [(b, max(lo, b * L), min(hi, (b + 1) * L)) for b in range(NB)
            if max(lo, b * L) < min(hi, (b + 1) * L)]


SPANS = [spans(k) for k in range(TT // 4)]
SPL = [sum(len(x) for x in SPANS[k % 2:k + 1:2]) for k in range(TT // 4)]


def hybrid_kernel(nc, dram, out):
    with ExitStack() as ctx:
        m = Mem(nc, ctx)
        s = {"ident": m.sb("ident", [P, P]), "t": None}
        s["rows"] = m.sb("rows", [P, 2 * P + E])
        s["rw"] = m.sb("rw", [P, E])
        s["ew"] = m.sb("ew", [P, E, P])
        s["eb"] = m.sb("eb", [E, P])
        s["wpT"] = m.sb("wpT", [P, P])
        with ExitStack() as outer:
            mo = Mem(nc, outer)
            s["xin"] = mo.sb("xin", [P, NB, L])
            s["u"] = mo.sb("u", [P, NB, L + TAPS - 1])
            with ExitStack() as inner:
                mi = Mem(nc, inner)
                for name, shape in (("par", [P, 8]), ("alog", [P, NS]), ("aneg", [P, NS]), ("wxT", [P, P]),
                                    ("wd", [P, P]), ("dd", [P, P]), ("gavg", [P, P]),
                                    ("state", [P, NS]), ("bcw", [P, 2 * NG, P])):
                    s[name] = mi.sb(name, shape)
                s["sel"] = mi.sb("sel", [P, GS * P], BF16)
                for name in ("xt", "delta", "dx"):
                    s[name] = mi.sb(name, [P, NB, L])
                with ExitStack() as part:
                    mp = Mem(nc, part)
                    s["scratch"] = mp.sb("scratch", [P, NB, L])
                    s["sel32"] = mp.sb("sel32", [P, GS * P])
                    first = ("xin", "gavg", "wxT", "par", "ident", "wd", "alog", "sel32", "bcw", "wpT", "rows",
                             "rw", "ew", "eb")
                    load_phase(nc, mp, dram, {k: s[k] for k in first})
                    stem_phase(nc, mp, s)
                with ExitStack() as part:
                    s["parts"] = Mem(nc, part).sb("parts", [P, 2 * NG, L], BF16)
                    for b in range(NB):
                        with ExitStack() as one:
                            split_phase(nc, Mem(nc, one), s, b)
                        with ExitStack() as one:
                            scan_phase(nc, Mem(nc, one), s, b)
            raise_t = Mem(nc, outer)
            token_out(nc, raise_t, s, dram, out)


def token_out(nc, mo, s, dram, out):
    s["t"] = mo.sb("t", [P, TT, P])
    for name in ("tok_hi", "tok_lo"):
        s[name] = mo.sb(name, [P, TT, P], F16)
    for name in ("xT_hi", "xT_lo"):
        s[name] = mo.sb(name, [P, TT * P], F16)
    with ExitStack() as part:
        token_phase(nc, Mem(nc, part), s)
    with ExitStack() as heads:
        mh = Mem(nc, heads)
        s["m_hi"] = mh.sb("m_hi", [P, H * P], F16)
        s["m_lo"] = mh.sb("m_lo", [P, H * P], F16)
        s["vo"] = mh.sb("vo", [P, H, P + 1])
        s["escale"] = mh.sb("escale", [P, H])
        s["ident16"] = mh.sb("ident16", [P, P], F16)
        with ExitStack() as part:
            mp = Mem(nc, part)
            s["wqkvT"] = mp.sb("wqkvT", [P, 3, H, P])
            s["wo"] = mp.sb("wo", [P, H, P])
            load_phase(nc, mp, dram, {k: s[k] for k in ("wqkvT", "wo")})
            weight_phase(nc, mp, s)
        with ExitStack() as part:
            attention_phase(nc, Mem(nc, part), s)
    with ExitStack() as part:
        expert_phase(nc, Mem(nc, part), s, out)


def _layout(i):
    import numpy as np

    g = {k: np.asarray(v) for k, v in i.items()}
    two = lambda name: [g[f"L0_conv_{d}_{name}"] for d in "fr"]
    f32 = np.float32
    par = np.zeros((P, 8), f32)
    par[:, 0] = g["L0_conv_bx"]
    for k, name in enumerate(("conv_b", "bd", "D")):
        par[:, 1 + k] = np.concatenate(two(name))
    par[:, 4:8] = np.concatenate(two("conv_w"))
    wd = np.zeros((P, P), f32)
    bcw = np.zeros((P, 2 * NG, P), f32)
    for d, w in enumerate(two("Wd")):
        wd[d * D2:(d + 1) * D2, d * D2:(d + 1) * D2] = w
    for which, name in enumerate(("WB", "WC")):
        for d, w in enumerate(two(name)):
            for k in range(NG):
                for row in (0, 64, 96):
                    lo = row + d * GS
                    bcw[d * D2:(d + 1) * D2, which * NG + k, lo:lo + GS] = w[:, k * GS:(k + 1) * GS]
    sel = np.zeros((P, GS, P), f32)
    for i_ in range(GS):
        for d in range(2):
            for row in (0, 64, 96):
                sel[row + d * GS + i_, i_, d * D2:(d + 1) * D2] = 1.0
    gavg = np.zeros((P, P), f32)
    for k in range(0, P, 4):
        gavg[k:k + 4, k:k + 4] = 0.25
    rows = np.concatenate([g["L0_conv_bp"], g["L1_attn_b_out"], g["L1_ffn_router_b"]])
    return {
        "xin": g["x"].reshape(NB, P, L).transpose(1, 0, 2),
        "wxT": g["L0_conv_Wx"].T, "wpT": g["L0_conv_Wp"].T, "par": par, "wd": wd,
        "alog": np.concatenate(two("Alog")), "bcw": bcw, "sel32": sel.reshape(P, GS * P), "gavg": gavg,
        "ident": np.eye(P, dtype=f32), "rows": np.broadcast_to(rows, (P, rows.size)),
        "wqkvT": g["L1_attn_w_qkv"].reshape(P, 3, H, P).transpose(3, 1, 2, 0),
        "wo": g["L1_attn_w_out"].reshape(H, P, P).transpose(1, 0, 2),
        "rw": g["L1_ffn_router_w"], "ew": g["L1_ffn_expert_w"].transpose(1, 0, 2), "eb": g["L1_ffn_expert_b"],
    }


def kernel(**inputs):
    import numpy as np
    from concourse import bacc
    from concourse.bass_utils import run_bass_kernel_spmd

    nc = bacc.Bacc("TRN2", target_bir_lowering=False, num_devices=1)
    arrays = {f"in_{k}": np.ascontiguousarray(v) for k, v in _layout(inputs).items()}
    dram = {k[3:]: nc.dram_tensor(k, a.shape, mybir.dt.from_np(a.dtype), kind="ExternalInput").ap()
            for k, a in arrays.items()}
    out = nc.dram_tensor("out", (NB, P, L), F32, kind="ExternalOutput").ap()
    hybrid_kernel(nc, dram, out)
    r = run_bass_kernel_spmd(nc, [arrays], core_ids=[0])
    return r.results[0]["out"].reshape(NB, P, 48, 48)
```

```python
from contextlib import ExitStack

import concourse.bass as bass
from concourse import mybir

ALU = mybir.AluOpType
ACT = mybir.ActivationFunctionType
AX = mybir.AxisListType
F32 = mybir.dt.float32
F16 = mybir.dt.float16
BF16 = mybir.dt.bfloat16
ds = bass.ds

P = 128
NB = 2
L = 48 * 48
NT = L // P
TT = NB * NT
W = 384
NC = L // W
D2 = P // 2
NS = 64
TAPS = 4
NG = 4
GS = NS // NG
NPAIR = NS // 2
NH = 4
H = 8
E = 8
SCALE = float(P) ** -0.5
BANK = 512


class Mem:

    def __init__(self, nc, ctx):
        self.nc, self.ctx = nc, ctx

    def sb(self, name, shape, dt=F32):
        return self.ctx.enter_context(self.nc.sbuf_tensor(name, shape, dt))

    def ps(self, name, shape, dt=F32):
        return self.ctx.enter_context(self.nc.psum_tensor(name, shape, dt))

    def sem(self, name):
        return self.ctx.enter_context(self.nc.semaphore(name))


def weight_phase(nc, m, s, dram, heads, others):
    wqkvT, wo = s["wqkvT"], s["wo"]
    m_hi, m_lo, vo, escale = s["m_hi"], s["m_lo"], s["vo"], s["escale"]
    dT = m.sb("w_less_c0", [P, 3, H, P])
    wps = m.ps("w_ps", [P, 4, 4, P])
    ext = m.sb("m_ext", [P, 2, H])
    big = m.sb("m_big", [P, H])
    allbig = m.sb("m_allbig", [P, H])
    inv = m.sb("m_inv", [P, H])
    mn = m.sb("m_norm", [P, H, P])
    d_in = m.sem("w_less_ready")
    w_ps = m.sem("w_ps_ready")
    step_in = m.sem("w_step")
    big_in = m.sem("m_big_ready")
    all_in = m.sem("m_allbig_ready")
    heads_loaded = m.sem("heads_loaded")
    loaded = m.sem("loaded")
    with nc.Block() as block:
        @block.sync
        def _(sp):
            for name in heads:
                sp.dma_start(s[name][:], dram[name]).then_inc(heads_loaded, 16)
            for name in others:
                sp.dma_start(s[name][:], dram[name]).then_inc(loaded, 16)
            sp.wait_ge(loaded, 16 * len(others))

        @block.vector
        def _(v):
            count = 0

            def link(ins):
                nonlocal count
                count += 1
                ins.then_inc(step_in, 1)
                v.wait_ge(step_in, count)

            v.wait_ge(heads_loaded, 16 * len(heads))
            for k in range(3):
                for h in range(H):
                    last = nc.vector.tensor_scalar(dT[:, k, h, :], wqkvT[:, k, h, :], wqkvT[:, k, h, 0:1],
                                                   None, ALU.subtract)
            last.then_inc(d_in, 1)
            nc.vector.memset(vo[:], 0.0)
            v.wait_ge(w_ps, 1)
            qk = wps[:, 0:2].rearrange("p a r e -> p (a r) e")
            nc.vector.tensor_reduce(ext[:, 0, :], qk, AX.X, ALU.max)
            link(nc.vector.tensor_reduce(ext[:, 1, :], qk, AX.X, ALU.min))
            nc.vector.scalar_tensor_tensor(out=big[:], in0=ext[:, 1, :], scalar=-1.0, in1=ext[:, 0, :],
                                           op0=ALU.mult, op1=ALU.max).then_inc(big_in, 1)
            v.wait_ge(all_in, 1)
            link(nc.vector.tensor_scalar(allbig[:], allbig[:], 1e-30, None, ALU.max))
            link(nc.vector.reciprocal(inv[:], allbig[:]))
            nc.vector.tensor_scalar(escale[:], allbig[:], SCALE, None, ALU.mult)
            for h in range(H):
                last = nc.vector.tensor_scalar(mn[:, h, :], wps[:, h // 4, h % 4, :], inv[:, h:h + 1], None,
                                               ALU.mult)
            link(last)
            link(nc.vector.tensor_copy(m_hi[:], mn[:].rearrange("p h e -> p (h e)")))
            nc.vector.tensor_tensor(m_lo[:], mn[:].rearrange("p h e -> p (h e)"), m_hi[:], ALU.subtract)
            v.wait_ge(w_ps, 2)
            nc.vector.tensor_copy(vo[:, :, 0:P], wps[:, 2:4].rearrange("p a r e -> p (a r) e"))
            nc.vector.memset(vo[0:1, :, P:P + 1], 1.0)
            nc.vector.tensor_copy(s["ident16"][:], s["ident"][:])

        @block.tensor
        def _(pe):
            pe.wait_ge(heads_loaded, 16 * len(heads))
            pe.wait_ge(d_in, 1)
            for h in range(H):
                mm = nc.tensor.matmul(wps[:, h // 4, h % 4, :], dT[:, 0, h, :], dT[:, 1, h, :],
                                      start=True, stop=True)
            mm.then_inc(w_ps, 1)
            for h in range(H):
                mm = nc.tensor.matmul(wps[:, 2 + h // 4, h % 4, :], dT[:, 2, h, :], wo[:, h, :],
                                      start=True, stop=True)
            mm.then_inc(w_ps, 1)

        @block.gpsimd
        def _(pool):
            pool.wait_ge(big_in, 1)
            nc.gpsimd.partition_all_reduce(allbig[:], big[:], P, bass.bass_isa.ReduceOp.max).then_inc(all_in, 1)


def stem_phase(nc, m, s):
    xin, u, xt, delta, dx = s["xin"], s["u"], s["xt"], s["delta"], s["dx"]
    par, ident = s["par"], s["ident"]
    bx, cb, bd, dd = (par[:, k:k + 1] for k in (0, 1, 2, 3))
    taps = [par[:, 4 + k:5 + k] for k in range(TAPS)]
    xg = delta
    stats = m.sb("gn_stats", [P, NB, NC, 6])
    mv = m.sb("gn_mv", [P, NB, 2])
    moments = m.sb("gn_moments", [P, NB, 2])
    group = m.sb("gn_group", [P, NB, 2])
    gvar = m.sb("gn_var", [P, NB])
    rstd = m.sb("gn_rstd", [P, NB])
    eps = m.sb("gn_eps", [P, 1])
    gps = m.ps("gn_ps", [P, BANK])
    fps = m.ps("fold_ps", [P, 3, BANK])
    fold_ps = m.sem("fold_ps_ready")
    folded = m.sem("folded")
    proj = m.ps("proj_ps", [P, 4, BANK])
    dve = m.sem("stem_dve")
    stats_in = m.sem("moments_ready")
    group_ps = m.sem("group_ready")
    var_in = m.sem("gvar_ready")
    std_in = m.sem("gstd_ready")
    xg_in = m.sem("xg_ready")
    u_ps = m.sem("u_ps_ready")
    u_in = m.sem("u_ready")
    v_in = m.sem("conv_ready")
    xt_in = m.sem("xt_ready")
    z_ps = m.sem("z_ps_ready")
    z_abs = m.sem("z_abs_ready")
    z_used = m.sem("z_ps_used")
    z_exp = m.sem("z_exp_ready")
    u1_in = m.sem("one_plus_exp_ready")
    ln_in = m.sem("ln_ready")
    delta_in = m.sem("delta_ready")
    const_in = m.sem("stem_const")
    with nc.Block() as block:
        @block.vector
        def _(v):
            count = 0

            def link(ins):
                nonlocal count
                count += 1
                ins.then_inc(dve, 1)
                v.wait_ge(dve, count)

            nc.vector.memset(eps[:], 1e-5).then_inc(const_in, 1)
            nc.vector.memset(u[:, :, 0:TAPS - 1], 0.0)
            for b in range(NB):
                for c in range(NC):
                    last = nc.vector.bn_stats(stats[:, b, c, :], xin[:, b, c * W:(c + 1) * W])
            link(last)
            for b in range(NB):
                last = nc.vector.bn_aggr(mv[:, b, :], stats[:, b, :, :])
            link(last)
            nc.vector.tensor_copy(moments[:, :, 0], mv[:, :, 0])
            link(nc.vector.tensor_tensor(moments[:, :, 1], mv[:, :, 0], mv[:, :, 0], ALU.mult))
            nc.vector.tensor_tensor(moments[:, :, 1], moments[:, :, 1], mv[:, :, 1],
                                    ALU.add).then_inc(stats_in, 1)
            v.wait_ge(group_ps, 1)
            link(nc.vector.tensor_copy(group[:], gps[:, 0:2 * NB].rearrange("p (b k) -> p b k", b=NB)))
            link(nc.vector.tensor_tensor(gvar[:], group[:, :, 0], group[:, :, 0], ALU.mult))
            nc.vector.tensor_tensor(gvar[:], group[:, :, 1], gvar[:], ALU.subtract).then_inc(var_in, 1)
            v.wait_ge(std_in, 1)
            link(nc.vector.reciprocal(rstd[:], gvar[:]))
            for b in range(NB):
                nc.vector.tensor_scalar(xg[:, b, :], xin[:, b, :], group[:, b, 0:1], rstd[:, b:b + 1],
                                        ALU.subtract, ALU.mult).then_inc(xg_in, 1)
            for b in range(NB):
                v.wait_ge(u_in, 2 * NC * (b + 1))
                link(nc.vector.tensor_scalar(xt[:, b, :], u[:, b, 0:L], taps[0], cb, ALU.mult, ALU.add))
                for k in range(1, TAPS):
                    ins = nc.vector.scalar_tensor_tensor(out=xt[:, b, :], in0=u[:, b, k:k + L], scalar=taps[k],
                                                         in1=xt[:, b, :], op0=ALU.mult, op1=ALU.add)
                    if k < TAPS - 1:
                        link(ins)
                ins.then_inc(v_in, 1)
            for b in range(NB):
                v.wait_ge(z_exp, b + 1)
                scr = s["scratch"][:, b, :]
                link(nc.vector.tensor_scalar(scr, dx[:, b, :], 1.0, None, ALU.add))
                nc.vector.scalar_tensor_tensor(out=dx[:, b, :], in0=scr, scalar=1.0, in1=dx[:, b, :],
                                               op0=ALU.subtract, op1=ALU.subtract).then_inc(u1_in, 1)
                v.wait_ge(u1_in, b + 1)
                link(nc.vector.tensor_tensor(delta[:, b, :], delta[:, b, :], dx[:, b, :], ALU.subtract))
            for b in range(NB):
                v.wait_ge(ln_in, b + 1)
                nc.vector.tensor_tensor(delta[:, b, :], delta[:, b, :], s["scratch"][:, b, :],
                                        ALU.add).then_inc(delta_in, 1)
            v.wait_ge(delta_in, NB)
            nc.vector.tensor_tensor(dx[:, NB - 1, :], delta[:, NB - 1, :], xt[:, NB - 1, :], ALU.mult)

        @block.tensor
        def _(pe):
            ew = s["ew"][:].rearrange("p e c -> p (e c)")
            for j in range(2):
                nc.tensor.matmul(fps[:, j, :], s["fold"][:], ew[:, j * BANK:(j + 1) * BANK], start=True, stop=True)
            nc.tensor.matmul(fps[:, 2, 0:E], s["fold"][:], s["rw"][:], start=True, stop=True).then_inc(fold_ps, 1)
            pe.wait_ge(stats_in, 1)
            nc.tensor.matmul(gps[:, 0:2 * NB], s["gavg"][:], moments[:].rearrange("p b k -> p (b k)"),
                             start=True, stop=True).then_inc(group_ps, 1)
            for b in range(NB):
                pe.wait_ge(xg_in, b + 1)
                for c in range(NC):
                    k = b * NC + c
                    if k >= 4:
                        pe.wait_ge(u_in, 2 * (k - 3))
                    nc.tensor.matmul(proj[:, k % 4, 0:W], s["wxT"][:], xg[:, b, c * W:(c + 1) * W],
                                     start=True, stop=True).then_inc(u_ps, 1)
            for b in range(NB):
                pe.wait_ge(xt_in, b + 1)
                for c in range(NC):
                    k = b * NC + c
                    if k < 4:
                        pe.wait_ge(u_in, 2 * NB * NC)
                    else:
                        pe.wait_ge(z_used, k - 3)
                    nc.tensor.matmul(proj[:, k % 4, 0:W], s["wd"][:], xt[:, b, c * W:(c + 1) * W],
                                     start=True, stop=True).then_inc(z_ps, 1)

        @block.scalar
        def _(act):
            act.wait_ge(fold_ps, 1)
            nc.scalar.copy(s["ew"][:].rearrange("p e c -> p (e c)"),
                           fps[:, 0:2, :].rearrange("p j c -> p (j c)")).then_inc(folded, 1)
            nc.scalar.copy(s["rw"][:], fps[:, 2, 0:E]).then_inc(folded, 1)
            act.wait_ge(folded, 2)
            nc.scalar.copy(s["ew"][0:1].rearrange("p e c -> p (e c)"), s["biases"][:, 0:E * P])
            nc.scalar.copy(s["rw"][0:1, :], s["biases"][:, E * P:E * P + E])
            act.wait_ge(const_in, 1)
            act.wait_ge(var_in, 1)
            nc.scalar.activation(gvar[:], gvar[:], ACT.Sqrt, bias=eps[:]).then_inc(std_in, 1)
            for b in range(NB):
                for c in range(NC):
                    k = b * NC + c
                    act.wait_ge(u_ps, k + 1)
                    lo = TAPS - 1 + c * W
                    nc.scalar.activation(u[0:D2, b, lo:lo + W], proj[0:D2, k % 4, 0:W], ACT.Identity,
                                         bias=bx[0:D2]).then_inc(u_in, 1)
                    hi = TAPS - 1 + L - 1 - c * W
                    nc.scalar.activation(u[D2:P, b, hi - W + 1:hi + 1][:, ::-1], proj[D2:P, k % 4, 0:W],
                                         ACT.Identity, bias=bx[D2:P]).then_inc(u_in, 1)

            def silu(b):
                act.wait_ge(v_in, b + 1)
                nc.scalar.activation(xt[:, b, :], xt[:, b, :], ACT.Silu).then_inc(xt_in, 1)

            def exp_abs(b):
                act.wait_ge(z_abs, NC * (b + 1))
                nc.scalar.activation(dx[:, b, :], dx[:, b, :], ACT.Exp, scale=-1.0).then_inc(z_exp, 1)

            silu(0)
            for b in range(NB):
                for c in range(NC):
                    k = b * NC + c
                    act.wait_ge(z_ps, k + 1)
                    cols = slice(c * W, (c + 1) * W)
                    nc.scalar.activation(dx[:, b, cols], proj[:, k % 4, 0:W], ACT.Abs,
                                         bias=bd).then_inc(z_abs, 1)
                    nc.scalar.activation(delta[:, b, cols], proj[:, k % 4, 0:W], ACT.Relu,
                                         bias=bd).then_inc(z_used, 1)
                if b + 1 < NB:
                    silu(b + 1)
                exp_abs(b)
            for b in range(NB):
                act.wait_ge(u1_in, b + 1)
                nc.scalar.activation(s["scratch"][:, b, :], s["scratch"][:, b, :], ACT.Ln).then_inc(ln_in, 1)
            nc.scalar.activation(s["alog"][:], s["alog"][:], ACT.Exp).then_inc(const_in, 1)
            act.wait_ge(const_in, 2)
            nc.scalar.mul(s["aneg"][:], s["alog"][:], -1.0)

        @block.gpsimd
        def _(pool):
            nc.gpsimd.tensor_scalar(s["dd"][:], ident[:], dd, None, ALU.mult)
            nc.gpsimd.tensor_copy(s["sel"][:], s["sel32"][:])
            for b in range(NB - 1):
                pool.wait_ge(delta_in, b + 1)
                nc.gpsimd.tensor_tensor(dx[:, b, :], delta[:, b, :], xt[:, b, :], ALU.mult)


def split_phase(nc, m, s, b):
    xt, parts = s["xt"], s["parts"]
    ps = m.ps(f"bc_ps{b}", [P, 4, 2, BANK])
    rest = m.sb(f"bc_rest{b}", [P, 4, 2, W])
    ps_ready = m.sem(f"bc_ps_ready{b}")
    first = m.sem(f"first_part{b}")
    rest_in = m.sem(f"rest_ready{b}")
    second = m.sem(f"second_part{b}")
    third = m.sem(f"third_part{b}")
    own_second = m.sem(f"own_second_part{b}")
    own_third = m.sem(f"own_third_part{b}")
    jobs = [(g, c) for g in range(2 * NG) for c in range(0, NC, 2)]

    def out(g, c, rows):
        return parts[rows, g, c * W:(c + 2) * W].rearrange("p (j w) -> p j w", j=2)

    with nc.Block() as block:
        @block.tensor
        def _(pe):
            for k, (g, c) in enumerate(jobs):
                if k >= 4:
                    pe.wait_ge(rest_in, k - 3)
                for j in range(2):
                    mm = nc.tensor.matmul(ps[:, k % 4, j, 0:W], s["bcw"][:, g, :],
                                          xt[:, b, (c + j) * W:(c + j + 1) * W], start=True, stop=True)
                mm.then_inc(ps_ready, 1)

        @block.scalar
        def _(act):
            def take_second(k):
                act.wait_ge(rest_in, k + 1)
                nc.scalar.copy(out(*jobs[k], slice(D2, P)), rest[D2:P, k % 4]).then_inc(second, 1)

            for k, (g, c) in enumerate(jobs):
                act.wait_ge(ps_ready, k + 1)
                nc.scalar.copy(out(g, c, slice(0, P)), ps[:, k % 4, :, 0:W]).then_inc(first, 1)
                if k >= 1 and (k - 1) % 4 != 3:
                    take_second(k - 1)

        @block.vector
        def _(v):
            rows = slice(96, P)
            for k in range(len(jobs) + 2):
                if k < len(jobs):
                    v.wait_ge(first, k + 1)
                    if k >= 4:
                        if k % 4 != 3:
                            v.wait_ge(third, 3 * (k // 4 - 1) + k % 4 + 1)
                        else:
                            v.wait_ge(own_third, k // 4)
                    nc.vector.tensor_tensor(rest[D2:P, k % 4], ps[D2:P, k % 4, :, 0:W],
                                            out(*jobs[k], slice(D2, P)), ALU.subtract).then_inc(rest_in, 1)
                if k >= 1 and (k - 1) % 4 == 3:
                    v.wait_ge(rest_in, k)
                    nc.vector.tensor_copy(out(*jobs[k - 1], slice(D2, P)), rest[D2:P, 3]).then_inc(own_second, 1)
                if k >= 2 and (k - 2) % 4 == 3:
                    v.wait_ge(own_second, (k - 2) // 4 + 1)
                    nc.vector.tensor_tensor(out(*jobs[k - 2], rows), rest[rows, 3], out(*jobs[k - 2], rows),
                                            ALU.subtract).then_inc(own_third, 1)

        @block.gpsimd
        def _(pool):
            rows = slice(96, P)
            for i, k in enumerate(k for k in range(len(jobs)) if k % 4 != 3):
                pool.wait_ge(second, i + 1)
                nc.gpsimd.tensor_tensor(out(*jobs[k], rows), rest[rows, k % 4], out(*jobs[k], rows),
                                        ALU.subtract).then_inc(third, 1)


def scan_phase(nc, m, s, b):
    xt, delta, dx, u = s["xt"], s["delta"], s["dx"], s["u"]
    parts, sel, aneg, state = s["parts"], s["sel"], s["aneg"], s["state"]
    bps = m.ps(f"b_ps{b}", [P, 2, BANK])
    cps = m.ps(f"c_ps{b}", [P, 2, BANK])
    da = m.ps(f"da_ps{b}", [P, 2, BANK])
    yps = m.ps(f"y_ps{b}", [P, 2, BANK])
    dbx = m.sb(f"dbx{b}", [P, 2, 2, W])
    hh = m.sb(f"h{b}", [P, NH, 2, W])
    csb = m.sb(f"c_sb{b}", [P, NH, 2, W])
    prod = m.sb(f"ch{b}", [P, 2, 2, W])
    names = ("b_ready", "c_ready", "c_copied", "da_ready", "dbx_ready", "scanned", "prod_ready",
             "state_saved", "summed", "y_taken")
    (b_ready, c_ready, c_copied, da_ready, dbx_ready, scanned, prod_ready,
     state_saved, summed, y_taken) = (m.sem(f"{n}{b}") for n in names)
    last_pair = NC * NPAIR - 1

    def pairs(engine, step):
        for c in range(NC):
            head = 1 + NH
            for q in range(head):
                step(c, q, q % NH, c * NPAIR + q)
            with engine.Fori(head // NH, NPAIR // NH - 1) as k:
                for i in range(1, NH + 1):
                    step(c, NH * k + i, i % NH, c * NPAIR + NH * k + i)
            for q in range(NPAIR - NH + 1, NPAIR):
                step(c, q, q % NH, c * NPAIR + q)

    with nc.Block() as block:
        @block.tensor
        def _(pe):
            def broadcast(c, q, n, base, ps, used, ready):
                if not (isinstance(n, int) and n < 1):
                    pe.wait_ge(used, n)
                if isinstance(q, int):
                    c, q = (c + 1, q - NPAIR) if q >= NPAIR else (c, q)
                    g, i = q // (GS // 2), q % (GS // 2)
                    rhs = parts[:, base + g, c * W:(c + 1) * W]
                    lhs = [sel[:, (2 * i + j) * P:(2 * i + j + 1) * P] for j in range(2)]
                else:
                    g, i = q // (GS // 2), q % (GS // 2)
                    flat = parts[:].rearrange("p g l -> p (g l)")
                    rhs = flat[:, ds(g * L + (base * L + c * W), W)]
                    lhs = [sel[:, ds(i * (2 * P) + j * P, P)] for j in range(2)]
                for j in range(2):
                    mm = nc.tensor.matmul(ps[:, j, 0:W], lhs[j], rhs, start=True, stop=True)
                mm.then_inc(ready, 1)

            def broadcast_b(c, q, n):
                if not (isinstance(n, int) and n > last_pair):
                    broadcast(c, q, n, 0, bps, dbx_ready, b_ready)

            def broadcast_c(c, q, n):
                if not (isinstance(n, int) and n > last_pair):
                    broadcast(c, q, n, NG, cps, c_copied, c_ready)

            def add(c, par, n, closes=False):
                pe.wait_ge(prod_ready, n + 1)
                for j in range(2):
                    mm = nc.tensor.matmul(yps[:, c % 2, 0:W], s["ident"][:], prod[:, par, j, :],
                                          start=False, stop=closes and j == 1)
                mm.then_inc(summed, 1)

            def step(c, q, buf, n):
                first = isinstance(q, int) and q == 0
                par = buf % 2
                broadcast_b(c, q + 2, n + 2)
                broadcast_c(c, q + 2, n + 2)
                if first:
                    if c >= 1:
                        add(c - 1, 1 - par, n - 1, closes=True)
                    if c >= 2:
                        pe.wait_ge(y_taken, 2 * (c - 1))
                    nc.tensor.matmul(yps[:, c % 2, 0:W], s["dd"][:], xt[:, b, c * W:(c + 1) * W],
                                     start=True, stop=False)
                else:
                    add(c, 1 - par, n - 1)

            broadcast_b(0, 0, 0)
            broadcast_c(0, 0, 0)
            broadcast_b(0, 1, 1)
            broadcast_c(0, 1, 1)
            pairs(pe, step)
            add(NC - 1, 1, last_pair, closes=True)

        @block.scalar
        def _(act):
            def take_y(c):
                act.wait_ge(summed, (c + 1) * NPAIR)
                lo, hi = TAPS - 1 + c * W, TAPS - 1 + L - 1 - c * W
                nc.scalar.copy(u[0:D2, b, lo:lo + W], yps[0:D2, c % 2, 0:W]).then_inc(y_taken, 1)
                nc.scalar.copy(u[D2:P, b, hi - W + 1:hi + 1][:, ::-1],
                               yps[D2:P, c % 2, 0:W]).then_inc(y_taken, 1)

            def step(c, q, buf, n):
                early = isinstance(n, int) and n < 1
                for j in range(2):
                    if not early:
                        act.wait_ge(scanned, 2 * n - 1 + j)
                    nc.scalar.activation(da[:, j, 0:W], delta[:, b, c * W:(c + 1) * W], ACT.Exp,
                                         scale=aneg[:, 2 * q + j:2 * q + j + 1] if isinstance(q, int)
                                         else aneg[:, ds(2 * q + j, 1)]).then_inc(da_ready, 1)
                    if j == 0:
                        act.wait_ge(c_ready, n + 1)
                        if not (isinstance(n, int) and n < NH):
                            act.wait_ge(prod_ready, n - NH + 1)
                        nc.scalar.copy(csb[:, buf], cps[:, :, 0:W]).then_inc(c_copied, 1)
                if c >= 1 and isinstance(q, int) and q == 3:
                    take_y(c - 1)

            pairs(act, step)
            take_y(NC - 1)

        @block.vector
        def _(v):
            def times_b(c, par, n):
                v.wait_ge(b_ready, n + 1)
                dxc = dx[:, b, c * W:(c + 1) * W].rearrange("p (o w) -> p o w", o=1).broadcast_to([P, 2, W])
                nc.vector.tensor_tensor(dbx[:, par], bps[:, :, 0:W], dxc, ALU.mult).then_inc(dbx_ready, 1)

            def step(c, q, buf, n):
                par = buf % 2
                if not (isinstance(n, int) and n < NH):
                    v.wait_ge(state_saved, n - NH + 1)
                v.wait_ge(dbx_ready, n + 1)
                for j in range(2):
                    v.wait_ge(da_ready, 2 * n + 1 + j)
                    initial = state[:, 2 * q + j:2 * q + j + 1] if isinstance(q, int) else \
                        state[:, ds(2 * q + j, 1)]
                    nc.vector.tensor_tensor_scan(hh[:, buf, j, :], da[:, j, 0:W], dbx[:, par, j, :],
                                                 initial if c else 0.0, ALU.mult,
                                                 ALU.add).then_inc(scanned, 1)
                    if j == 0 and not (isinstance(n, int) and n == last_pair):
                        if not (isinstance(n, int) and n < 1):
                            v.wait_ge(scanned, 2 * n)
                        times_b(c + (isinstance(q, int) and q == NPAIR - 1), 1 - par, n + 1)

            times_b(0, 0, 0)
            pairs(v, step)

        @block.gpsimd
        def _(pool):
            def step(c, q, buf, n):
                par = buf % 2
                pool.wait_ge(scanned, 2 * n + 2)
                pool.wait_ge(c_copied, n + 1)
                if not (isinstance(n, int) and n < 2):
                    pool.wait_ge(summed, n - 1)
                nc.gpsimd.tensor_tensor(prod[:, par], hh[:, buf], csb[:, buf], ALU.mult).then_inc(prod_ready, 1)
                keep = state[:, 2 * q:2 * q + 2] if isinstance(q, int) else state[:, ds(2 * q, 2)]
                nc.gpsimd.tensor_copy(keep, hh[:, buf, :, W - 1]).then_inc(state_saved, 1)

            pairs(pool, step)


def token_phase(nc, m, s):
    t, u, xin, ident = s["t"], s["u"], s["xin"], s["ident"]
    tok_hi, tok_lo, xT_hi, xT_lo = s["tok_hi"], s["tok_lo"], s["xT_hi"], s["xT_lo"]
    tps = m.ps("t_ps", [P, 4, 4, P])
    xps = m.ps("xh_ps", [P, 4, 4, P])
    stats = m.sb("ln1_stats", [P, TT, 6])
    mv = m.sb("ln1_mv", [P, TT, 2])
    std = m.sb("ln1_std", [P, TT])
    rstd = m.sb("ln1_rstd", [P, TT])
    shift = m.sb("ln1_shift", [P, TT])
    eps = m.sb("ln1_eps", [P, 1])
    xh = m.sb("xh", [P, TT, P])
    const_in = m.sem("ln1_const")
    t_ps = m.sem("t_ps_ready")
    t_in = m.sem("t_ready")
    st = m.sem("ln1_stats_ready")
    mv_in = m.sem("ln1_mv_ready")
    std_in = m.sem("ln1_std_ready")
    rstd_in = m.sem("ln1_rstd_ready")
    shift_in = m.sem("ln1_shift_ready")
    xh_in = m.sem("xh_ready")
    hi_in = m.sem("tok_hi_ready")
    x_ps = m.sem("xT_ps_ready")
    xhi = m.sem("xT_hi_ready")
    xlo = m.sem("xT_lo_ready")
    NQ = TT // 4

    def row(lo):
        return s["rows"][:, lo:lo + P].rearrange("p (o c) -> p o c", o=1).broadcast_to([P, 4, P])

    def four(k):
        return slice(4 * k, 4 * k + 4)

    with nc.Block() as block:
        @block.tensor
        def _(pe):
            for k in range(NQ + 2):
                if k < NQ:
                    if k >= 4:
                        pe.wait_ge(t_in, k - 3)
                    for r in range(4):
                        b, i = divmod(4 * k + r, NT)
                        lo = TAPS - 1 + i * P
                        nc.tensor.matmul(tps[:, k % 4, r, :], u[:, b, lo:lo + P], s["wpT"][:],
                                         start=True, stop=False)
                        mm = nc.tensor.matmul(tps[:, k % 4, r, :], xin[:, b, i * P:(i + 1) * P], ident[:],
                                              start=False, stop=True)
                    mm.then_inc(t_ps, 1)
                if k >= 2:
                    j = k - 2
                    pe.wait_ge(const_in, 2)
                    pe.wait_ge(xh_in, j + 1)
                    if j >= 4:
                        pe.wait_ge(xlo, j - 3)
                    for r in range(4):
                        mm = nc.tensor.transpose(xps[:, j % 4, r, :], xh[:, 4 * j + r, :], ident[:])
                    mm.then_inc(x_ps, 1)

        @block.vector
        def _(v):
            nc.vector.memset(eps[:], 1e-5).then_inc(const_in, 1)
            nc.vector.memset(xh[:, :, 0], 1.0).then_inc(const_in, 1)
            for k in range(NQ + 3):
                if k < NQ:
                    v.wait_ge(t_ps, k + 1)
                    nc.vector.tensor_tensor(t[:, four(k), :], tps[:, k % 4], row(0), ALU.add).then_inc(t_in, 1)
                if 1 <= k <= NQ:
                    j = k - 1
                    v.wait_ge(std_in, j + 1)
                    nc.vector.reciprocal(rstd[:, four(j)], std[:, four(j)]).then_inc(rstd_in, 1)
                if k < NQ:
                    v.wait_ge(t_in, k + 1)
                    for i in range(4 * k, 4 * k + 4):
                        last = nc.vector.bn_stats(stats[:, i, :], t[:, i, :])
                    last.then_inc(st, 1)
                if 1 <= k <= NQ:
                    v.wait_ge(rstd_in, j + 1)
                    nc.vector.scalar_tensor_tensor(out=shift[:, four(j)], in0=mv[:, four(j), 0], scalar=-1.0,
                                                   in1=rstd[:, four(j)], op0=ALU.mult,
                                                   op1=ALU.mult).then_inc(shift_in, 1)
                if k < NQ:
                    v.wait_ge(st, k + 1)
                    for i in range(4 * k, 4 * k + 4):
                        last = nc.vector.bn_aggr(mv[:, i, :], stats[:, i, :])
                    last.then_inc(mv_in, 1)
                if k >= 3:
                    j = k - 3
                    v.wait_ge(xhi, j + 1)
                    cols = slice(4 * j * P, (4 * j + 4) * P)
                    nc.vector.tensor_tensor(xT_lo[:, cols], xps[:, j % 4].rearrange("p r t -> p (r t)"),
                                            xT_hi[:, cols], ALU.subtract).then_inc(xlo, 1)

        @block.scalar
        def _(act):
            act.wait_ge(const_in, 1)
            for k in range(NQ + 3):
                if k < NQ:
                    act.wait_ge(mv_in, k + 1)
                    nc.scalar.activation(std[:, four(k)], mv[:, four(k), 1], ACT.Sqrt,
                                         bias=eps[:]).then_inc(std_in, 1)
                if k >= 3:
                    j = k - 3
                    act.wait_ge(x_ps, j + 1)
                    nc.scalar.copy(xT_hi[:, 4 * j * P:(4 * j + 4) * P],
                                   xps[:, j % 4].rearrange("p r t -> p (r t)")).then_inc(xhi, 1)
                if 1 <= k <= NQ:
                    j = k - 1
                    act.wait_ge(shift_in, j + 1)
                    for i in range(4 * j, 4 * j + 4):
                        last = nc.scalar.activation(xh[:, i, 1:P], t[:, i, 1:P], ACT.Identity,
                                                    scale=rstd[:, i:i + 1], bias=shift[:, i:i + 1])
                    last.then_inc(xh_in, 1)
                    act.wait_ge(const_in, 2)
                    act.wait_ge(xh_in, j + 1)
                    nc.scalar.copy(tok_hi[:, four(j), :], xh[:, four(j), :]).then_inc(hi_in, 1)

        @block.gpsimd
        def _(pool):
            for k in range(NQ):
                pool.wait_ge(xh_in, k + 1)
                nc.gpsimd.tensor_tensor(t[:, four(k), :], t[:, four(k), :], row(P), ALU.add)
                pool.wait_ge(hi_in, k + 1)
                nc.gpsimd.tensor_tensor(tok_lo[:, four(k), :], xh[:, four(k), :], tok_hi[:, four(k), :],
                                        ALU.subtract)


def attention_phase(nc, m, s):
    t, xT_hi, xT_lo, tok_hi, tok_lo = s["t"], s["xT_hi"], s["xT_lo"], s["tok_hi"], s["tok_lo"]
    m_hi, m_lo, vo, escale, ident16 = s["m_hi"], s["m_lo"], s["vo"], s["escale"], s["ident16"]
    stats, mv = s["ln2_stats"], s["ln2_mv"]
    NF = NB * H * NC
    KP = NT // 2
    RING = 8
    TC = W // P
    q_hi = m.sb("q_hi", [P, RING * W], F16)
    q_lo = m.sb("q_lo", [P, RING * W], F16)
    p32 = m.sb("p32", [P, 3, 2, W])
    p_hi = m.sb("p_hi", [P, 3, 2, W], F16)
    p_lo = m.sb("p_lo", [P, 3, 2, W], F16)
    z = m.sb("z", [P, 2, W])
    mxp = m.sb("max_parts", [P, 2, TC, 3])
    mx_sb = m.sb("maximum", [P, 2, TC])
    mneg = m.sb("max_neg", [P, 2, TC], F16)
    rl = m.sb("sum_inv", [P, 2, TC])
    scale = m.sb("head_scale", [P, 2])
    sps = m.ps("s_ps", [P, 2, 2, BANK])
    mps = m.ps("max_ps", [P, 2, BANK])
    pvps = m.ps("pv_ps", [P, BANK])
    misc = m.ps("misc_ps", [P, BANK])
    OW = P + 1
    vo_flat = vo[:].rearrange("p h o -> p (h o)")
    t_flat = t[:].rearrange("p t c -> p (t c)")
    tok_hi, tok_lo = (x[:].rearrange("p t c -> p (t c)") for x in (tok_hi, tok_lo))
    out_ps = misc[:, 0:TC * OW].rearrange("p (t o) -> p t o", t=TC)

    q_ps = m.sem("q_ps_ready")
    qh_in = m.sem("q_hi_ready")
    ql_in = m.sem("q_lo_ready")
    s_ready = m.sem("scores_ready")
    exp_hi = m.sem("exp_hi_ready")
    exp_in = m.sem("exp_ready")
    lo_in = m.sem("p_lo_ready")
    pv_done = m.sem("pv_done")
    z_in = m.sem("z_ready")
    mx_ps = m.sem("max_ps_ready")
    mx_part = m.sem("max_part_ready")
    mx_in = m.sem("max_ready")
    mneg_in = m.sem("max_neg_ready")
    row_ps = m.sem("max_row_ps_ready")
    row_in = m.sem("max_row_ready")
    o_ps = m.sem("out_ps_ready")
    rl_in = m.sem("sum_inv_ready")
    o_in = m.sem("out_added")
    scale_in = m.sem("head_scale_ready")
    stats_in = m.sem("ln2_stats_ready")

    def image(F):
        return F // (H * NC)

    def at(F):
        return (F % RING) * W

    def tile(F):
        return image(F) * NT + (F % NC) * TC

    def head(F):
        return (F // NC) % H

    LEAD = 4
    MLEAD = 2

    def schedule(engine, body):
        def turn(G, half, proj=True, mx=True, row=True, main=True, prev=True):
            body(G, half, proj, mx, row, main, prev)

        def turns(first, end, **parts):
            if first < end:
                with engine.Fori(first // 2, end // 2) as k:
                    turn(2 * k, 0, **parts)
                    turn(2 * k + 1, 1, **parts)

        for G in range(2):
            turn(G, G, mx=False, row=False, main=False, prev=False)
        turns(2, MLEAD, mx=False, row=False, main=False, prev=False)
        turn(MLEAD, 0, row=False, main=False, prev=False)
        turn(MLEAD + 1, 1, main=False, prev=False)
        turns(MLEAD + 2, LEAD, main=False, prev=False)
        turn(LEAD, 0, prev=False)
        turn(LEAD + 1, 1)
        turns(LEAD + 2, NF)
        turns(NF, NF + MLEAD, proj=False)
        turn(NF + MLEAD, 0, proj=False, mx=False)
        turn(NF + MLEAD + 1, 1, proj=False, mx=False, row=False)
        turns(NF + MLEAD + 2, NF + LEAD, proj=False, mx=False, row=False)

    def max_bank(half, kp, main):
        return mps if main or (half + kp) % 2 == 0 else sps[:, 0]

    def wait(engine, sem, value):
        if not isinstance(value, int) or value > 0:
            engine.wait_ge(sem, value)

    with nc.Block() as block:
        @block.tensor
        def _(pe):
            def misc_free(G, user, proj, row, prev):
                if user == "out" and row:
                    pe.wait_ge(row_in, G - MLEAD)
                elif user != "proj" and proj:
                    pe.wait_ge(qh_in, G + 1)
                    pe.wait_ge(ql_in, G + 1)
                elif prev:
                    wait(pe, o_in, G - LEAD - 1)
                    if isinstance(G, int) and G == LEAD + 1:
                        pe.wait_ge(row_in, G - MLEAD - 1)
                elif row:
                    pe.wait_ge(row_in, G - MLEAD - 1)
                    pe.wait_ge(ql_in, G)
                elif not (isinstance(G, int) and G == 0):
                    pe.wait_ge(qh_in, G)
                    pe.wait_ge(ql_in, G)

            def project(G):
                cols = ds(image(G) * L + (G % NC) * W, W)
                w = ds(head(G) * P, P)
                nc.tensor.matmul(misc[:, 0:W], m_hi[:, w], xT_hi[:, cols], start=True, stop=False)
                nc.tensor.matmul(misc[:, 0:W], m_hi[:, w], xT_lo[:, cols], start=False, stop=False)
                nc.tensor.matmul(misc[:, 0:W], m_lo[:, w], xT_hi[:, cols], start=False,
                                 stop=True).then_inc(q_ps, 1)

            def weighted_sum(kp, F, n):
                if kp == 0:
                    wait(pe, z_in, F)
                wait(pe, lo_in, n + 1)
                k0 = image(F) * NT * P
                for j in range(2):
                    keys = ds(k0 + (2 * kp + j) * P, P)
                    hi, lo = p_hi[:, kp % 3, j, :], p_lo[:, kp % 3, j, :]
                    nc.tensor.matmul(pvps[:, 0:W], tok_hi[:, keys], hi, start=kp + j == 0, stop=False)
                    nc.tensor.matmul(pvps[:, 0:W], tok_hi[:, keys], lo, start=False, stop=False)
                    mm = nc.tensor.matmul(pvps[:, 0:W], tok_lo[:, keys], hi, start=False,
                                          stop=kp == KP - 1 and j == 1)
                mm.then_inc(pv_done, 1)

            def output(F, par):
                pe.wait_ge(z_in, F + 1)
                w = ds(head(F) * OW, OW)
                for i in range(TC):
                    mm = nc.tensor.matmul(out_ps[:, i, :], z[:, par, i * P:(i + 1) * P], vo_flat[:, w],
                                          start=True, stop=True)
                mm.then_inc(o_ps, 1)

            def body(G, half, proj, mx, row, main, prev):
                F, M, R = G - LEAD, G - MLEAD, G - MLEAD - 1
                for kp in range(KP):
                    n, nm = F * KP + kp, M * KP + kp
                    if kp == 0 and proj:
                        misc_free(G, "proj", proj, row, prev)
                        project(G)
                    if kp == 3 and row:
                        misc_free(G, "row", proj, row, prev)
                        pe.wait_ge(mneg_in, R + 1)
                        for i in range(TC):
                            mm = nc.tensor.matmul(misc[0:1, i * P:(i + 1) * P], mneg[:, 1 - half, i:i + 1],
                                                  ident16[:], start=True, stop=True)
                        mm.then_inc(row_ps, 1)
                    if kp == 5 and prev:
                        misc_free(G, "out", proj, row, prev)
                        output(F - 1, 1 - half)
                    if main:
                        if kp == 0:
                            pe.wait_ge(row_in, F + 1)
                            if isinstance(G, int) and G == LEAD:
                                pe.wait_ge(mx_part, MLEAD * KP)
                        wait(pe, exp_in, n - 1)
                        q = ds(at(F), W)
                        k0 = image(F) * L
                        sb = (half + kp) % 2
                        for j in range(2):
                            keys = ds(k0 + (2 * kp + j) * P, P)
                            o = sps[:, sb, j, 0:W]
                            nc.tensor.matmul(o, xT_hi[:, keys], q_hi[:, q], start=True, stop=False)
                            nc.tensor.matmul(o, xT_hi[:, keys], q_lo[:, q], start=False, stop=False)
                            mm = nc.tensor.matmul(o, xT_lo[:, keys], q_hi[:, q], start=False, stop=True)
                        mm.then_inc(s_ready, 1)
                    if mx:
                        if kp == 0:
                            pe.wait_ge(qh_in, M + 1)
                        wait(pe, mx_part, nm if main or isinstance(G, int) and G == MLEAD and kp == 0
                             else nm - 1)
                        q = ds(at(M) + (kp // 3) * P, P)
                        for j in range(2):
                            keys = ds(image(M) * L + (2 * (kp % 3) + j) * W, W)
                            mm = nc.tensor.matmul(max_bank(half, kp, main)[:, j, 0:W], q_hi[:, q], xT_hi[:, keys],
                                                  start=True, stop=True)
                        mm.then_inc(mx_ps, 1)
                    if kp >= 2 and main:
                        weighted_sum(kp - 2, F, n - 2)
                    elif kp < 2 and prev:
                        weighted_sum(kp + KP - 2, F - 1, n - 2)

            schedule(pe, body)
            for kp in (KP - 2, KP - 1):
                weighted_sum(kp, NF - 1, (NF - 1) * KP + kp)
            pe.wait_ge(o_in, NF - 1)
            output(NF - 1, 1)

        @block.scalar
        def _(act):
            def take_z(F, par):
                act.wait_ge(pv_done, (F + 1) * KP)
                wait(act, o_ps, F)
                nc.scalar.copy(z[:, par, :], pvps[:, 0:W]).then_inc(z_in, 1)

            def body(G, half, proj, mx, row, main, prev):
                F, R = G - LEAD, G - MLEAD - 1
                if main:
                    nc.scalar.copy(scale[:, half:half + 1], escale[:, ds(head(F), 1)]).then_inc(scale_in, 1)
                    act.wait_ge(scale_in, F + 1)
                for kp in range(KP):
                    if kp == 0 and proj:
                        act.wait_ge(q_ps, G + 1)
                        nc.scalar.copy(q_hi[:, ds(at(G), W)], misc[:, 0:W]).then_inc(qh_in, 1)
                    if kp == 2 and prev:
                        take_z(F - 1, 1 - half)
                    if kp == 3 and row:
                        act.wait_ge(row_ps, R + 1)
                        nc.scalar.copy(q_hi[0:1, ds(at(R), W)], misc[0:1, 0:W]).then_inc(row_in, 1)
                    if main:
                        n = F * KP + kp
                        src = sps[:, (half + kp) % 2, :, 0:W]
                        sc = scale[:, half:half + 1]
                        act.wait_ge(s_ready, n + 1)
                        wait(act, pv_done, n - 2)
                        nc.scalar.activation(p_hi[:, kp % 3], src, ACT.Exp, scale=sc).then_inc(exp_hi, 1)
                        wait(act, lo_in, n - 2)
                        nc.scalar.activation(p32[:, kp % 3], src, ACT.Exp, scale=sc).then_inc(exp_in, 1)

            schedule(act, body)
            take_z(NF - 1, 1)

        @block.vector
        def _(v):
            def add_output(F, par):
                v.wait_ge(o_ps, F + 1)
                nc.vector.reciprocal(rl[:, par, :], out_ps[:, :, P]).then_inc(rl_in, 1)
                v.wait_ge(rl_in, F + 1)
                for i in range(TC):
                    tok = t_flat[:, ds((tile(F) + i) * P, P)]
                    ins = nc.vector.scalar_tensor_tensor(out=tok, in0=out_ps[:, i, 0:P],
                                                         scalar=rl[:, par, i:i + 1], in1=tok,
                                                         op0=ALU.mult, op1=ALU.add)
                ins.then_inc(o_in, 1)

            def statistics(kp, last_turn):
                tiles = range(2 * kp, 2 * kp + 2)
                if last_turn:
                    tiles = range(NT + 2 * kp, NT + 2 * kp + 2)
                    if kp == 6:
                        v.wait_ge(o_in, NF - 1)
                        tiles = range(TT - 2 * TC, TT - TC)
                    elif kp > 6:
                        tiles = ()
                if last_turn and kp == 0:
                    v.wait_ge(o_in, NF - 2)
                elif kp == 0:
                    v.wait_ge(o_in, NF // 2)
                for i in tiles:
                    nc.vector.bn_stats(stats[:, i, :], t[:, i, :]).then_inc(stats_in, 1)

            def body(G, half, proj, mx, row, main, prev):
                F, M, R = G - LEAD, G - MLEAD, G - MLEAD - 1
                if row:
                    v.wait_ge(mx_part, (R + 1) * KP)
                    nc.vector.tensor_reduce(mx_sb[:, 1 - half, :], mxp[:, 1 - half], AX.X,
                                            ALU.max).then_inc(mx_in, 1)
                    v.wait_ge(mx_in, R + 1)
                    nc.vector.tensor_scalar(mneg[:, 1 - half, :], mx_sb[:, 1 - half, :], -1.0, None,
                                            ALU.mult).then_inc(mneg_in, 1)
                for kp in range(KP):
                    n, nm = F * KP + kp, M * KP + kp
                    if mx:
                        v.wait_ge(mx_ps, nm + 1)
                        nc.vector.tensor_reduce(mxp[:, half, kp // 3, kp % 3:kp % 3 + 1],
                                                max_bank(half, kp, main)[:, :, 0:W],
                                                AX.XY, ALU.max).then_inc(mx_part, 1)
                    if kp == 0 and proj:
                        v.wait_ge(qh_in, G + 1)
                        cols = ds(at(G), W)
                        nc.vector.tensor_tensor(q_lo[:, cols], misc[:, 0:W], q_hi[:, cols],
                                                ALU.subtract).then_inc(ql_in, 1)
                    if kp == 5 and prev:
                        add_output(F - 1, 1 - half)
                    if main:
                        v.wait_ge(exp_in, n + 1)
                        wait(v, pv_done, n - 2)
                        nc.vector.tensor_tensor(p_lo[:, kp % 3], p32[:, kp % 3], p_hi[:, kp % 3],
                                                ALU.subtract).then_inc(lo_in, 1)
                    if isinstance(G, int) and G >= NF + MLEAD:
                        statistics(kp, G > NF + MLEAD)

            schedule(v, body)
            v.wait_ge(stats_in, TT - TC)
            for i in range(TT - TC):
                nc.vector.bn_aggr(mv[:, i, :], stats[:, i, :])
            add_output(NF - 1, 1)


def expert_phase(nc, m, s, out):
    t, ident = s["t"], s["ident"]
    stats, mv = s["ln2_stats"], s["ln2_mv"]
    std = m.sb("ln2_std", [P, TT])
    rstd = m.sb("ln2_rstd", [P, TT])
    eps = m.sb("ln2_eps", [P, 1])
    x2 = m.sb("x2", [P, TT, P])
    x2T = m.sb("x2T", [P, TT, P])
    lg = m.sb("logits", [P, TT, E])
    order = m.sb("order", [P, E])
    rest = m.sb("logits_rest", [P, TT, E])
    cand = m.sb("candidates", [P, TT, E])
    best = [m.sb(f"best{j}", [P, TT, E]) for j in range(2)]
    top = m.sb("top", [P, TT])
    first = m.sb("first", [P, TT])
    ex = m.sb("router_exp", [P, TT, E])
    den = m.sb("top_sum", [P, TT])
    wgt = m.sb("weight", [P, TT, E])
    ob = m.sb("out_sb", [P, 2, 4 * P])
    aps = m.ps("a_ps", [P, 2, BANK])
    rps = m.ps("router_ps", [P, 2, BANK])
    eps_ps = m.ps("expert_ps", [P, 2, 2, BANK])
    dve = m.sem("expert_dve")
    mv_in = m.sem("ln2_mv_ready")
    std_in = m.sem("ln2_std_ready")
    x2_in = m.sem("x2_ready")
    a_ps = m.sem("a_ps_ready")
    a_used = m.sem("a_ps_used")
    r_ps = m.sem("router_ps_ready")
    sub_in = m.sem("less_top_ready")
    ex_in = m.sem("router_exp_ready")
    w_in = m.sem("weight_ready")
    e_ps = m.sem("expert_ps_ready")
    e_used = m.sem("expert_added")
    stored = [m.sem(f"stored{j}") for j in range(2)]
    NQ = TT // 4
    CUT = 5
    PARTS = ((0, 4 * CUT), (4 * CUT, TT))
    with nc.Block() as block:
        @block.vector
        def _(v):
            count = 0

            def link(ins):
                nonlocal count
                count += 1
                ins.then_inc(dve, 1)
                v.wait_ge(dve, count)

            nc.vector.memset(eps[:], 1e-5)
            nc.vector.memset(x2[:, :, 0], 1.0)
            for k in range(TT - W // P, TT):
                last = nc.vector.bn_stats(stats[:, k, :], t[:, k, :])
            link(last)
            for k in range(TT - W // P, TT):
                last = nc.vector.bn_aggr(mv[:, k, :], stats[:, k, :])
            last.then_inc(mv_in, 1)
            v.wait_ge(std_in, 1)
            link(nc.vector.reciprocal(rstd[:], std[:]))
            for k in range(TT):
                ins = nc.vector.tensor_scalar(x2[:, k, 1:P], t[:, k, 1:P], mv[:, k, 0:1], rstd[:, k:k + 1],
                                              ALU.subtract, ALU.mult)
                if k % 4 == 3:
                    ins.then_inc(x2_in, 1)
            for e in range(E):
                last = nc.vector.memset(order[:, e:e + 1], float(E - e))
            link(last)
            def combine(k):
                for e in range(E):
                    if e % 4 == 0:
                        v.wait_ge(e_ps, k + 1 + e // 4)
                    for r in range(2):
                        if e:
                            v.wait_ge(e_used, k * E + 2 * e + r - 1)
                        nc.vector.scalar_tensor_tensor(
                            out=t[:, k + r, :], in0=eps_ps[:, r, e // 4, (e % 4) * P:(e % 4 + 1) * P],
                            scalar=wgt[:, k + r, e:e + 1], in1=t[:, k + r, :], op0=ALU.mult,
                            op1=ALU.add).then_inc(e_used, 1)

            for g, (lo, hi) in enumerate(PARTS):
                tiles = slice(lo, hi)
                rows = [P, hi - lo, E]
                v.wait_ge(r_ps, g + 1)
                link(nc.vector.tensor_copy(lg[:, tiles], rps[:, g, lo * E:hi * E].rearrange("p (t e) -> p t e", e=E)))
                orderb = order[:].rearrange("p (o c) -> p o c", o=1).broadcast_to(rows)
                topb, firstb, denb = (x[:, tiles].rearrange("p (t o) -> p t o", o=1).broadcast_to(rows)
                                      for x in (top, first, den))
                exg, candg = ex[:, tiles], cand[:, tiles]

                def find_best(logits, j):
                    link(nc.vector.tensor_reduce(top[:, tiles], logits[:, tiles], AX.X, ALU.max))
                    if j == 0:
                        nc.vector.tensor_tensor(exg, lg[:, tiles], topb, ALU.subtract).then_inc(sub_in, 1)
                    link(nc.vector.tensor_tensor(candg, logits[:, tiles], topb, ALU.is_equal))
                    link(nc.vector.tensor_tensor(candg, candg, orderb, ALU.mult))
                    link(nc.vector.tensor_reduce(first[:, tiles], candg, AX.X, ALU.max))
                    link(nc.vector.tensor_tensor(best[j][:, tiles], candg, firstb, ALU.is_equal))

                find_best(lg, 0)
                link(nc.vector.scalar_tensor_tensor(out=rest[:, tiles], in0=best[0][:, tiles], scalar=-3e38,
                                                    in1=lg[:, tiles], op0=ALU.mult, op1=ALU.add))
                find_best(rest, 1)
                link(nc.vector.tensor_tensor(candg, best[0][:, tiles], best[1][:, tiles], ALU.add))
                v.wait_ge(ex_in, g + 1)
                link(nc.vector.tensor_tensor(exg, exg, candg, ALU.mult))
                link(nc.vector.tensor_reduce(den[:, tiles], exg, AX.X, ALU.add))
                link(nc.vector.reciprocal(den[:, tiles], den[:, tiles]))
                nc.vector.tensor_tensor(wgt[:, tiles], exg, denb, ALU.mult).then_inc(w_in, 1)
                if g == 0:
                    v.wait_ge(w_in, 1)
                    combine(0)
            v.wait_ge(w_in, len(PARTS))
            for k in range(2, TT, 2):
                combine(k)

        @block.tensor
        def _(pe):
            def route(g):
                pe.wait_ge(a_used, g + 1)
                for k in range(4 * g, 4 * g + 4):
                    mm = nc.tensor.matmul(rps[:, int(g >= CUT), k * E:(k + 1) * E], x2T[:, k, :], s["rw"][:],
                                          start=True, stop=True)
                if g in (CUT - 1, NQ - 1):
                    mm.then_inc(r_ps, 1)

            def experts(k):
                for j in range(2):
                    if k >= 2:
                        pe.wait_ge(e_used, (k - 2) * E + (j + 1) * E)
                    for r in range(2):
                        mm = nc.tensor.matmul(eps_ps[:, r, j, :], x2T[:, k + r, :],
                                              s["ew"][:, 4 * j:4 * j + 4, :].rearrange("p e c -> p (e c)"),
                                              start=True, stop=True)
                    mm.then_inc(e_ps, 1)

            def result(k):
                pe.wait_ge(a_used, NQ + max(k - 1, 0))
                pe.wait_ge(e_used, (4 * k + 4) * E)
                for r in range(4):
                    i = 4 * k + r
                    mm = nc.tensor.transpose(aps[:, k % 2, r * P:(r + 1) * P], t[:, i, :], ident[:])
                mm.then_inc(a_ps, 1)

            for k in range(NQ):
                pe.wait_ge(x2_in, k + 1)
                if k >= 2:
                    pe.wait_ge(a_used, k - 1)
                for r in range(4):
                    mm = nc.tensor.transpose(aps[:, k % 2, r * P:(r + 1) * P], x2[:, 4 * k + r, :], ident[:])
                mm.then_inc(a_ps, 1)
                if k >= 1:
                    route(k - 1)
                if k == CUT:
                    experts(0)
            route(NQ - 1)
            for k in range(2, TT, 2):
                experts(k)
                if k % 4 == 0:
                    result(k // 4 - 1)
            result(NQ - 1)

        @block.scalar
        def _(act):
            act.wait_ge(mv_in, 1)
            nc.scalar.activation(std[:], mv[:, :, 1], ACT.Sqrt, bias=eps[:]).then_inc(std_in, 1)
            for k in range(NQ):
                act.wait_ge(a_ps, k + 1)
                nc.scalar.copy(x2T[:, 4 * k:4 * k + 4, :].rearrange("p r t -> p (r t)"),
                               aps[:, k % 2, :]).then_inc(a_used, 1)
                if k in (CUT + 1, NQ - 1):
                    g = k // (NQ - 1)
                    lo, hi = PARTS[g]
                    act.wait_ge(sub_in, g + 1)
                    nc.scalar.activation(ex[:, lo:hi], ex[:, lo:hi], ACT.Exp).then_inc(ex_in, 1)
            for k in range(NQ):
                act.wait_ge(a_ps, NQ + k + 1)
                if k >= 2:
                    act.wait_ge(stored[k % 2], 16 * SPL[k - 2])
                nc.scalar.copy(ob[:, k % 2, :], aps[:, k % 2, :]).then_inc(a_used, 1)

        @block.sync
        def _(sp):
            for k in range(NQ):
                sp.wait_ge(a_used, NQ + k + 1)
                for b, lo, hi in SPANS[k]:
                    off = lo - 4 * k * P
                    sp.dma_start(out[b, :, lo - b * L:hi - b * L],
                                 ob[:, k % 2, off:off + hi - lo]).then_inc(stored[k % 2], 16)
            for k in (NQ - 2, NQ - 1):
                sp.wait_ge(stored[k % 2], 16 * SPL[k])


def spans(k):
    lo, hi = 4 * k * P, (4 * k + 4) * P
    return [(b, max(lo, b * L), min(hi, (b + 1) * L)) for b in range(NB)
            if max(lo, b * L) < min(hi, (b + 1) * L)]


SPANS = [spans(k) for k in range(TT // 4)]
SPL = [sum(len(x) for x in SPANS[k % 2:k + 1:2]) for k in range(TT // 4)]


def hybrid_kernel(nc, dram, out):
    with ExitStack() as ctx:
        m = Mem(nc, ctx)
        s = {"ident": m.sb("ident", [P, P])}
        s["rows"] = m.sb("rows", [P, 2 * P])
        s["rw"] = m.sb("rw", [P, E])
        s["ew"] = m.sb("ew", [P, E, P])
        s["biases"] = m.sb("biases", [1, E * P + E])
        s["fold"] = m.sb("fold", [P, P])
        s["wpT"] = m.sb("wpT", [P, P])
        s["m_hi"] = m.sb("m_hi", [P, H * P], F16)
        s["m_lo"] = m.sb("m_lo", [P, H * P], F16)
        s["vo"] = m.sb("vo", [P, H, P + 1])
        s["escale"] = m.sb("escale", [P, H])
        s["ident16"] = m.sb("ident16", [P, P], F16)
        with ExitStack() as outer:
            mo = Mem(nc, outer)
            s["xin"] = mo.sb("xin", [P, NB, L])
            s["u"] = mo.sb("u", [P, NB, L + TAPS - 1])
            with ExitStack() as inner:
                mi = Mem(nc, inner)
                for name, shape in (("par", [P, 8]), ("alog", [P, NS]), ("aneg", [P, NS]), ("wxT", [P, P]),
                                    ("wd", [P, P]), ("dd", [P, P]), ("gavg", [P, P]),
                                    ("state", [P, NS]), ("bcw", [P, 2 * NG, P])):
                    s[name] = mi.sb(name, shape)
                s["sel"] = mi.sb("sel", [P, GS * P], BF16)
                for name in ("xt", "delta", "dx"):
                    s[name] = mi.sb(name, [P, NB, L])
                with ExitStack() as part:
                    mp = Mem(nc, part)
                    s["scratch"] = mp.sb("scratch", [P, NB, L])
                    s["sel32"] = mp.sb("sel32", [P, GS * P])
                    with ExitStack() as start:
                        mw = Mem(nc, start)
                        s["wqkvT"] = mw.sb("wqkvT", [P, 3, H, P])
                        s["wo"] = mw.sb("wo", [P, H, P])
                        weight_phase(nc, mw, s, dram, ("wqkvT", "wo", "ident"),
                                     ("xin", "gavg", "wxT", "par", "wd", "alog", "sel32", "bcw", "wpT", "rows",
                                      "rw", "ew", "biases", "fold"))
                    stem_phase(nc, mp, s)
                with ExitStack() as part:
                    s["parts"] = Mem(nc, part).sb("parts", [P, 2 * NG, L], BF16)
                    for b in range(NB):
                        with ExitStack() as one:
                            split_phase(nc, Mem(nc, one), s, b)
                        with ExitStack() as one:
                            scan_phase(nc, Mem(nc, one), s, b)
            token_out(nc, Mem(nc, outer), s, out)


def token_out(nc, mo, s, out):
    s["t"] = mo.sb("t", [P, TT, P])
    for name in ("tok_hi", "tok_lo"):
        s[name] = mo.sb(name, [P, TT, P], F16)
    for name in ("xT_hi", "xT_lo"):
        s[name] = mo.sb(name, [P, TT * P], F16)
    with ExitStack() as part:
        token_phase(nc, Mem(nc, part), s)
    s["ln2_stats"] = mo.sb("ln2_stats", [P, TT, 6])
    s["ln2_mv"] = mo.sb("ln2_mv", [P, TT, 2])
    with ExitStack() as part:
        attention_phase(nc, Mem(nc, part), s)
    with ExitStack() as part:
        expert_phase(nc, Mem(nc, part), s, out)


def _layout(i):
    import numpy as np

    g = {k: np.asarray(v) for k, v in i.items()}
    two = lambda name: [g[f"L0_conv_{d}_{name}"] for d in "fr"]
    f32 = np.float32
    par = np.zeros((P, 8), f32)
    par[:, 0] = g["L0_conv_bx"]
    for k, name in enumerate(("conv_b", "bd", "D")):
        par[:, 1 + k] = np.concatenate(two(name))
    par[:, 4:8] = np.concatenate(two("conv_w"))
    wd = np.zeros((P, P), f32)
    bcw = np.zeros((P, 2 * NG, P), f32)
    for d, w in enumerate(two("Wd")):
        wd[d * D2:(d + 1) * D2, d * D2:(d + 1) * D2] = w
    for which, name in enumerate(("WB", "WC")):
        for d, w in enumerate(two(name)):
            for k in range(NG):
                for row in (0, 64, 96):
                    lo = row + d * GS
                    bcw[d * D2:(d + 1) * D2, which * NG + k, lo:lo + GS] = w[:, k * GS:(k + 1) * GS]
    sel = np.zeros((P, GS, P), f32)
    for i_ in range(GS):
        for d in range(2):
            for row in (0, 64, 96):
                sel[row + d * GS + i_, i_, d * D2:(d + 1) * D2] = 1.0
    gavg = np.zeros((P, P), f32)
    for k in range(0, P, 4):
        gavg[k:k + 4, k:k + 4] = 0.25
    fold = np.eye(P, dtype=f32)
    fold[0, :] = -1.0
    rows = np.concatenate([g["L0_conv_bp"], g["L1_attn_b_out"]])
    return {
        "xin": g["x"].reshape(NB, P, L).transpose(1, 0, 2),
        "wxT": g["L0_conv_Wx"].T, "wpT": g["L0_conv_Wp"].T, "par": par, "wd": wd,
        "alog": np.concatenate(two("Alog")), "bcw": bcw, "sel32": sel.reshape(P, GS * P), "gavg": gavg,
        "ident": np.eye(P, dtype=f32), "rows": np.broadcast_to(rows, (P, rows.size)),
        "wqkvT": g["L1_attn_w_qkv"].reshape(P, 3, H, P).transpose(3, 1, 2, 0),
        "wo": g["L1_attn_w_out"].reshape(H, P, P).transpose(1, 0, 2),
        "rw": g["L1_ffn_router_w"], "ew": g["L1_ffn_expert_w"].transpose(1, 0, 2), 
        "biases": np.concatenate([g["L1_ffn_expert_b"].reshape(-1), g["L1_ffn_router_b"]])[None], "fold": fold,
    }


def kernel(**inputs):
    import numpy as np
    from concourse import bacc
    from concourse.bass_utils import run_bass_kernel_spmd

    nc = bacc.Bacc("TRN2", target_bir_lowering=False, num_devices=1)
    arrays = {f"in_{k}": np.ascontiguousarray(v) for k, v in _layout(inputs).items()}
    dram = {k[3:]: nc.dram_tensor(k, a.shape, mybir.dt.from_np(a.dtype), kind="ExternalInput").ap()
            for k, a in arrays.items()}
    out = nc.dram_tensor("out", (NB, P, L), F32, kind="ExternalOutput").ap()
    hybrid_kernel(nc, dram, out)
    r = run_bass_kernel_spmd(nc, [arrays], core_ids=[0])
    return r.results[0]["out"].reshape(NB, P, 48, 48)
```
